# Optimizing a Trainium2 kernel written in Bass

```python
import numpy as np
import jax
import jax.numpy as jnp

def _softmax(x, axis=-1):
    return jax.nn.softmax(x, axis=axis)

def _gelu(x):
    return jax.nn.gelu(x, approximate=True)

def _silu(x):
    return jax.nn.silu(x)

def _sigmoid(x):
    return jax.nn.sigmoid(x)

def _layernorm(x, axis=-1, eps=1e-05):
    m = jnp.mean(x, axis=axis, keepdims=True)
    v = jnp.var(x, axis=axis, keepdims=True)
    return (x - m) / jnp.sqrt(v + eps)

def _scatter_add(tgt, idx, src, axis=0):
    return tgt.at[idx].add(src)

def _segment_sum(src, seg, n):
    return jax.ops.segment_sum(src, seg, n)
kernel_name = 'mk_cond_resid_d4_seqx_r2_3bbf1d'

def setup_inputs(seed: int=0):
    np.random.seed(seed)
    _w = jnp.asarray

    def _rec_inputs():
        import jax
        import jax.numpy as jnp
        _rk = jax.random.key(seed)
        x = -0.000125 + 0.9999 * jax.random.normal(jax.random.fold_in(_rk, 1), (128, 128, 2048), jnp.float32)
        _lenS = 128 - jax.random.randint(jax.random.fold_in(_rk, 7), (128,), 0, max(1, 128 // 4) + 1, jnp.int32)
        _lenS2 = 128 - jax.random.randint(jax.random.fold_in(_rk, 8), (128,), 0, max(1, 128 // 4) + 1, jnp.int32)
        cond_128 = 0.0061147 + 1.02565 * jax.random.normal(jax.random.fold_in(_rk, 11), (128, 128), jnp.float32)
        fside_S_0 = -0.022604 + 0.987366 * jax.random.normal(jax.random.fold_in(_rk, 12), (128,), jnp.float32)
        return (x, cond_128, fside_S_0)
    x, cond_128, fside_S_0 = _rec_inputs()

    def _L0_cond_setup():
        import jax, jax.numpy as jnp
        import numpy as np
        from jax import lax
        N, C_IN, L = (32, 128, 2048)
        C_OUT, K, GROUPS = (128, 9, 4)
        C_DIM, PAD, STRIDE = (128, 4, 1)
        key = jax.random.key(seed)
        k1, k2, k3, k4, k5 = jax.random.split(key, 5)
        x = jax.random.normal(k1, (N, C_IN, L), dtype=jnp.float32)
        c = jax.random.normal(k2, (N, C_DIM), dtype=jnp.float32)
        weight = jax.random.normal(k3, (C_OUT, C_IN // GROUPS, K), dtype=jnp.float32)
        c_weight = jax.random.normal(k4, (C_OUT, C_DIM), dtype=jnp.float32)
        bias = jax.random.normal(k5, (C_OUT,), dtype=jnp.float32)
        return {'x': x, 'c': c, 'weight': weight, 'c_weight': c_weight, 'bias': bias}
    _L0_cond_all = _L0_cond_setup()
    _L0_cond_in = {k: v for k, v in _L0_cond_all.items() if k in ('weight', 'c_weight')}
    del _L0_cond_all

    def _L1_cond_setup():
        import jax, jax.numpy as jnp
        import numpy as np
        K = 8
        T = 1.0
        D_EMBD = 128
        IN_C = 128
        OUT_C = 128
        BS = 32
        H = 2048
        HID = 128
        key = jax.random.key(seed)
        ks = jax.random.split(key, 10)
        s = lambda fan_in: 1.0 / np.sqrt(fan_in)
        return {'x': jax.random.normal(ks[0], (BS, IN_C, H), dtype=jnp.float32), 'embedding': jax.random.normal(ks[1], (BS, D_EMBD), dtype=jnp.float32), 'W0': jax.random.normal(ks[2], (D_EMBD, HID), dtype=jnp.float32) * s(D_EMBD), 'b0': jnp.zeros((HID,), dtype=jnp.float32), 'W1': jax.random.normal(ks[3], (HID, HID), dtype=jnp.float32) * s(HID), 'b1': jnp.zeros((HID,), dtype=jnp.float32), 'W2': jax.random.normal(ks[4], (HID, K), dtype=jnp.float32) * s(HID), 'b2': jnp.zeros((K,), dtype=jnp.float32), 'weight': jax.random.normal(ks[5], (K, OUT_C, IN_C, 1), dtype=jnp.float32) * s(IN_C), 'bias_k': jax.random.normal(ks[6], (K, OUT_C), dtype=jnp.float32) * 0.1}
    _L1_cond_all = _L1_cond_setup()
    _L1_cond_in = {k: v for k, v in _L1_cond_all.items() if k in ('W0', 'b0', 'W1', 'b1', 'W2', 'b2', 'weight', 'bias_k')}
    del _L1_cond_all

    def _L2_cond_setup():
        import jax, jax.numpy as jnp
        import numpy as np
        from jax import lax
        N, C_IN, L = (32, 128, 2048)
        C_OUT, K, GROUPS = (128, 9, 4)
        C_DIM, PAD, STRIDE = (128, 4, 1)
        key = jax.random.key(seed)
        k1, k2, k3, k4, k5 = jax.random.split(key, 5)
        x = jax.random.normal(k1, (N, C_IN, L), dtype=jnp.float32)
        c = jax.random.normal(k2, (N, C_DIM), dtype=jnp.float32)
        weight = jax.random.normal(k3, (C_OUT, C_IN // GROUPS, K), dtype=jnp.float32)
        c_weight = jax.random.normal(k4, (C_OUT, C_DIM), dtype=jnp.float32)
        bias = jax.random.normal(k5, (C_OUT,), dtype=jnp.float32)
        return {'x': x, 'c': c, 'weight': weight, 'c_weight': c_weight, 'bias': bias}
    _L2_cond_all = _L2_cond_setup()
    _L2_cond_in = {k: v for k, v in _L2_cond_all.items() if k in ('weight', 'c_weight')}
    del _L2_cond_all

    def _L3_cond_setup():
        import jax, jax.numpy as jnp
        import numpy as np
        K = 8
        T = 1.0
        D_EMBD = 128
        IN_C = 128
        OUT_C = 128
        BS = 32
        H = 2048
        HID = 128
        key = jax.random.key(seed)
        ks = jax.random.split(key, 10)
        s = lambda fan_in: 1.0 / np.sqrt(fan_in)
        return {'x': jax.random.normal(ks[0], (BS, IN_C, H), dtype=jnp.float32), 'embedding': jax.random.normal(ks[1], (BS, D_EMBD), dtype=jnp.float32), 'W0': jax.random.normal(ks[2], (D_EMBD, HID), dtype=jnp.float32) * s(D_EMBD), 'b0': jnp.zeros((HID,), dtype=jnp.float32), 'W1': jax.random.normal(ks[3], (HID, HID), dtype=jnp.float32) * s(HID), 'b1': jnp.zeros((HID,), dtype=jnp.float32), 'W2': jax.random.normal(ks[4], (HID, K), dtype=jnp.float32) * s(HID), 'b2': jnp.zeros((K,), dtype=jnp.float32), 'weight': jax.random.normal(ks[5], (K, OUT_C, IN_C, 1), dtype=jnp.float32) * s(IN_C), 'bias_k': jax.random.normal(ks[6], (K, OUT_C), dtype=jnp.float32) * 0.1}
    _L3_cond_all = _L3_cond_setup()
    _L3_cond_in = {k: v for k, v in _L3_cond_all.items() if k in ('W0', 'b0', 'W1', 'b1', 'W2', 'b2', 'weight', 'bias_k')}
    del _L3_cond_all
    return {'x': x, 'cond_128': cond_128, 'fside_S_0': fside_S_0, 'L0_cond_weight': _L0_cond_in['weight'], 'L0_cond_c_weight': _L0_cond_in['c_weight'], 'L1_cond_W0': _L1_cond_in['W0'], 'L1_cond_b0': _L1_cond_in['b0'], 'L1_cond_W1': _L1_cond_in['W1'], 'L1_cond_b1': _L1_cond_in['b1'], 'L1_cond_W2': _L1_cond_in['W2'], 'L1_cond_b2': _L1_cond_in['b2'], 'L1_cond_weight': _L1_cond_in['weight'], 'L1_cond_bias_k': _L1_cond_in['bias_k'], 'L2_cond_weight': _L2_cond_in['weight'], 'L2_cond_c_weight': _L2_cond_in['c_weight'], 'L3_cond_W0': _L3_cond_in['W0'], 'L3_cond_b0': _L3_cond_in['b0'], 'L3_cond_W1': _L3_cond_in['W1'], 'L3_cond_b1': _L3_cond_in['b1'], 'L3_cond_W2': _L3_cond_in['W2'], 'L3_cond_b2': _L3_cond_in['b2'], 'L3_cond_weight': _L3_cond_in['weight'], 'L3_cond_bias_k': _L3_cond_in['bias_k']}

def reference(x, cond_128, fside_S_0, L0_cond_weight, L0_cond_c_weight, L1_cond_W0, L1_cond_b0, L1_cond_W1, L1_cond_b1, L1_cond_W2, L1_cond_b2, L1_cond_weight, L1_cond_bias_k, L2_cond_weight, L2_cond_c_weight, L3_cond_W0, L3_cond_b0, L3_cond_W1, L3_cond_b1, L3_cond_W2, L3_cond_b2, L3_cond_weight, L3_cond_bias_k):
    import jax
    import jax.numpy as jnp

    def _L0_cond_ref(x, c, weight, c_weight, bias):
        import jax, jax.numpy as jnp
        import numpy as np
        from jax import lax
        N, C_IN, L = (32, 128, 2048)
        C_OUT, K, GROUPS = (128, 9, 4)
        C_DIM, PAD, STRIDE = (128, 4, 1)
        out = lax.conv_general_dilated(x, weight, window_strides=(STRIDE,), padding=[(PAD, PAD)], dimension_numbers=('NCH', 'OIH', 'NCH'), feature_group_count=GROUPS)
        ctx = jnp.einsum('nd,od->no', c, c_weight)
        out = out + ctx[:, :, None] + bias[None, :, None]
        return out

    def _L1_cond_ref(x, embedding, W0, b0, W1, b1, W2, b2, weight, bias_k):
        import jax, jax.numpy as jnp
        import numpy as np
        K = 8
        T = 1.0
        D_EMBD = 128
        IN_C = 128
        OUT_C = 128
        BS = 32
        H = 2048
        HID = 128
        h = jax.nn.gelu(embedding @ W0 + b0, approximate=False)
        h = jax.nn.gelu(h @ W1 + b1, approximate=False)
        att = jax.nn.softmax((h @ W2 + b2) / T, axis=-1)
        agg_w = jnp.einsum('bk,koi->boi', att, weight[..., 0])
        agg_b = att @ bias_k
        out = jnp.einsum('boi,bih->boh', agg_w, x) + agg_b[:, :, None]
        return out

    def _L2_cond_ref(x, c, weight, c_weight, bias):
        import jax, jax.numpy as jnp
        import numpy as np
        from jax import lax
        N, C_IN, L = (32, 128, 2048)
        C_OUT, K, GROUPS = (128, 9, 4)
        C_DIM, PAD, STRIDE = (128, 4, 1)
        out = lax.conv_general_dilated(x, weight, window_strides=(STRIDE,), padding=[(PAD, PAD)], dimension_numbers=('NCH', 'OIH', 'NCH'), feature_group_count=GROUPS)
        ctx = jnp.einsum('nd,od->no', c, c_weight)
        out = out + ctx[:, :, None] + bias[None, :, None]
        return out

    def _L3_cond_ref(x, embedding, W0, b0, W1, b1, W2, b2, weight, bias_k):
        import jax, jax.numpy as jnp
        import numpy as np
        K = 8
        T = 1.0
        D_EMBD = 128
        IN_C = 128
        OUT_C = 128
        BS = 32
        H = 2048
        HID = 128
        h = jax.nn.gelu(embedding @ W0 + b0, approximate=False)
        h = jax.nn.gelu(h @ W1 + b1, approximate=False)
        att = jax.nn.softmax((h @ W2 + b2) / T, axis=-1)
        agg_w = jnp.einsum('bk,koi->boi', att, weight[..., 0])
        agg_b = att @ bias_k
        out = jnp.einsum('boi,bih->boh', agg_w, x) + agg_b[:, :, None]
        return out
    x = x + _L0_cond_ref(x, cond_128, L0_cond_weight, L0_cond_c_weight, fside_S_0)
    x = x + _L1_cond_ref(x, cond_128, L1_cond_W0, L1_cond_b0, L1_cond_W1, L1_cond_b1, L1_cond_W2, L1_cond_b2, L1_cond_weight, L1_cond_bias_k)
    x = x + _L2_cond_ref(x, cond_128, L2_cond_weight, L2_cond_c_weight, fside_S_0)
    x = x + _L3_cond_ref(x, cond_128, L3_cond_W0, L3_cond_b0, L3_cond_W1, L3_cond_b1, L3_cond_W2, L3_cond_b2, L3_cond_weight, L3_cond_bias_k)
    return x

_drawn_inputs = setup_inputs


def setup_inputs(seed=0):
    import zlib

    import numpy as np

    out = dict(_drawn_inputs(seed))
    spreads = {'L1_cond_b0': (0.0, 0.611),
     'L1_cond_b1': (0.0, 0.436),
     'L1_cond_b2': (0.0, 0.346),
     'L3_cond_b0': (0.0, 0.53),
     'L3_cond_b1': (0.0, 0.357),
     'L3_cond_b2': (0.0, 0.275)}
    factors = {'L1_cond_bias_k': 35.953, 'L3_cond_bias_k': 64.0}
    for name, (base, spread) in spreads.items():
        noise = np.random.default_rng([zlib.crc32(name.encode()), seed]).standard_normal(out[name].shape)
        drawn = base * np.exp(spread * noise) if base else spread * noise
        out[name] = jnp.asarray(drawn.astype(out[name].dtype))
    for name, factor in factors.items():
        out[name] = (out[name] * factor).astype(out[name].dtype)
    return out
```

```python
from contextlib import ExitStack

import concourse.bass as bass
from concourse import mybir

F32 = mybir.dt.float32
ALU = mybir.AluOpType
ACT = mybir.ActivationFunctionType
AX = mybir.AxisListType

P = 128
GROUPS = 4
CG = P // GROUPS
PH = 4
HALVES = 2
BANK = 512
PB = 2
CONV_BIAS, MIX1_BIAS, MIX3_BIAS, BIASES = (0, 1), 2, 6, 7
KIND_ORDER = (1, 2, 0, 3)


def conditioned_layers(nc, x, emb_t, eye, fside, conv_w, ctx_w, mlp, out):
    B, C, L = x.shape
    S = L // PH
    R = S // 2
    TAPS = conv_w[0].shape[0]
    HALO = TAPS // 2
    PAIRS = B // PB
    EXPERTS = mlp[0]["w2"].shape[1]
    CHUNK = 4 * BANK
    CHUNKS = 2 * P * P // CHUNK
    assert C == P and B == P and S == BANK and PB * R == BANK and TAPS == 2 * PH + 1 and PAIRS > 4

    mix_dram = [nc.dram_tensor(f"mix_dram{m}", (B, P * P), F32).ap() for m in range(2)]

    with ExitStack() as ctx:
        def sb(name, shape):
            return ctx.enter_context(nc.sbuf_tensor(name, shape, F32))

        def sem(name):
            return ctx.enter_context(nc.semaphore(name))

        xin = sb("xin", [P, PB, L])
        xph = [sb(f"xph{v}", [P, GROUPS, PB, S + 2]) for v in range(2)]
        dif = [sb(f"dif{v}", [P, 4, GROUPS, PB, R]) for v in range(2)]
        y = [sb(f"y{v}", [P, PH, PB, S]) for v in range(2)]
        outb = sb("outb", [P, PB, L])
        half = sb("half", [P, 2, 2, BANK])
        mid = sb("mid", [P, 2, 2, BANK])
        wino = [sb(f"wino{v}", [P, 4, GROUPS, PH, CG]) for v in range(2)]
        mixw = [sb(f"mixw{m}", [P, PB, P]) for m in range(2)]
        bias_table = sb("bias_table", [P, B, BIASES])
        bias_now = sb("bias_now", [P, 2, PB, BIASES])
        psum = ctx.enter_context(nc.psum_tensor("psum", [P, HALVES, 4, BANK], F32))

        blocks = [y[v][:].rearrange("p j b s -> p (j b s)")[:, 0:3 * BANK].rearrange(
            "p (m g j o) -> p m g j o", m=3, g=GROUPS, j=PH) for v in range(2)]
        room = [y[v][:].rearrange("p j b s -> p (j b s)")[:, 3 * BANK:] for v in range(2)]
        experts = [dif[v][:].rearrange("p k g b r -> p (k g b r)") for v in range(2)]
        EXP_COLS = experts[0].shape[1]
        stage_out = outb[:]

        used = [0, 0]

        def carve(v, cols):
            used[v] += cols
            return room[v][:, used[v] - cols:used[v]]

        emb_sb = carve(0, B)
        eye_sb = carve(0, P)
        ones = carve(0, P)
        fside_sb = carve(0, 1)
        ctx_sb = [carve(0, P) for _ in range(2)]
        par, hid = [], []
        for m in range(2):
            par.append({"w0": carve(1, P), "w1": carve(1, P), "w2": carve(1, EXPERTS), "b0": carve(1, 1),
                        "b1": carve(1, 1), "b2": carve(1, EXPERTS), "bias_k": carve(1, P)})
            hid.append({"h": carve(0, P),
                        "h1": carve(1, P), "logit": carve(0, EXPERTS), "nmax": carve(0, 1), "exp": carve(0, EXPERTS),
                        "sum": carve(0, 1), "inv": carve(0, 1), "att": carve(0, EXPERTS), "att_t": carve(1, P)})

        par_loaded = sem("par_loaded")
        taps_loaded = sem("taps_loaded")
        taps_cleared = sem("taps_cleared")
        experts_loaded = [sem(f"experts_loaded{v}") for v in range(2)]
        wino_step = sem("wino_step")
        wino_ready = sem("wino_ready")
        filled = sem("filled")
        mlp_pe = sem("mlp_pe")
        mlp_act = sem("mlp_act")
        max_ready = sem("max_ready")
        mlp_dve = sem("mlp_dve")
        bias_pe = sem("bias_pe")
        bias_ready = sem("bias_ready")
        agg_pe = sem("agg_pe")
        agg_act = sem("agg_act")
        agg_dve = sem("agg_dve")
        agg_stored = [sem(f"agg_stored{v}") for v in range(2)]

        bias_picked = sem("bias_picked")
        x_loaded = sem("x_loaded")
        phased_act = sem("phased_act")
        phased_dve = sem("phased_dve")
        dif0_ready = sem("dif0_ready")
        dif2_ready = sem("dif2_ready")
        kind_done = sem("kind_done")
        half_ready = sem("half_ready")
        mid_ready = sem("mid_ready")
        y_ready = sem("y_ready")
        mix1_loaded = sem("mix1_loaded")
        mix3_loaded = sem("mix3_loaded")
        mix1_done = sem("mix1_done")
        xph1_ready = sem("xph1_ready")
        mix3_done = sem("mix3_done")
        out_ready = sem("out_ready")
        out_stored = [sem(f"out_stored{b}") for b in range(PB)]

        def stage0(i, j):
            return j if isinstance(i, int) and i == 0 else 8 * i - 4 + j

        def stage2(n, j):
            return 8 * n + 8 + j - (4 if isinstance(n, int) and n == PAIRS - 1 else 0)

        def pipeline(eng, step):
            step(0)
            step(1)
            with eng.Fori(2, PAIRS - 2) as i:
                step(i)
            step(PAIRS - 2)
            step(PAIRS - 1)
            step(PAIRS)

        def is_front(i):
            return not (isinstance(i, int) and i >= PAIRS)

        def is_back(i):
            return not (isinstance(i, int) and i < 1)

        def has(i, ahead):
            return not (isinstance(i, int) and i + ahead >= PAIRS)

        COPIES = [(p, g) for p in range(PH) for g in range(GROUPS)]
        ACT_COPIES, DVE_COPIES = COPIES[:8], COPIES[8:]

        def phase_copy(p, g):
            dst = xph[0][CG * p:CG * (p + 1), g, :, 1:S + 1]
            src = xin[CG * g:CG * (g + 1), :, p:p + PH * (S - 1) + 1:PH]
            return dst, src

        block = ctx.enter_context(nc.Block())

        @block.sync
        def _(sp):
            for v in range(2):
                sp.wait_ge(taps_cleared, v + 1)
                for p in range(PH):
                    for j in range(PH):
                        for m in range(3):
                            k = PH * (m - 1) + p - j + HALO
                            if 0 <= k < TAPS:
                                sp.dma_start(blocks[v][CG * p:CG * (p + 1), m, :, j, :],
                                             conv_w[v][k]).then_inc(taps_loaded, 16)

            def load_x(n):
                if not (isinstance(n, int) and n == 0):
                    sp.wait_ge(phased_act, n)
                    sp.wait_ge(phased_dve, n)
                for b in range(PB):
                    sp.dma_start(xin[:, b, :], x[PB * n + b]).then_inc(x_loaded, 16)

            def load_mix(m, n):
                if not (isinstance(n, int) and n == 0):
                    if m == 0:
                        sp.wait_ge(mix1_done, PB * GROUPS * n)
                    else:
                        sp.wait_ge(mix3_done, PB * n)
                for b in range(PB):
                    src = mix_dram[m].rearrange("b (i o) -> b i o", i=P)
                    sp.dma_start(mixw[m][:, b, :], src[PB * n + b]).then_inc((mix1_loaded, mix3_loaded)[m], 16)

            load_x(0)
            for chunk in range(CHUNKS):
                sp.wait_ge(agg_act, chunk + 1)
                sp.wait_ge(agg_dve, chunk + 1)
                m, at = divmod(chunk * CHUNK, P * P)
                sp.dma_start(mix_dram[m][:, at:at + CHUNK], stage_out[:, chunk % 2, :]).then_inc(agg_stored[chunk % 2], 16)
            load_x(1)
            for v in range(2):
                sp.wait_ge(agg_stored[v], 16 * CHUNKS // 2)
            load_mix(0, 0)
            load_mix(1, 0)

            def step(i):
                if has(i, 2):
                    load_x(i + 2)
                if has(i, 1):
                    load_mix(0, i + 1)
                if is_back(i):
                    for b in range(PB):
                        sp.wait_ge(out_ready, PB * (i - 1) + b + 1)
                        sp.dma_start(out[PB * (i - 1) + b], outb[:, b, :]).then_inc(out_stored[b], 16)
                    if has(i, 0):
                        load_mix(1, i)

            pipeline(sp, step)
            for b in range(PB):
                sp.wait_ge(out_stored[b], 16 * PAIRS)

        @block.gpsimd
        def _(pool):
            pool.dma_start(emb_sb, emb_t).then_inc(par_loaded, 16)
            pool.dma_start(eye_sb, eye).then_inc(par_loaded, 16)
            for m in range(2):
                for name in ("w0", "w1", "w2", "b0", "b1"):
                    pool.dma_start(par[m][name], mlp[m][name]).then_inc(par_loaded, 16)
                pool.dma_start(par[m]["b2"][0:1, :], mlp[m]["b2"]).then_inc(par_loaded, 16)
                pool.dma_start(par[m]["bias_k"][0:EXPERTS, :], mlp[m]["bias_k"]).then_inc(par_loaded, 16)
            pool.dma_start(fside_sb, fside).then_inc(par_loaded, 16)
            for v in range(2):
                pool.dma_start(ctx_sb[v], ctx_w[v]).then_inc(par_loaded, 16)
            lot = 0
            for m in range(2):
                for at in range(0, P * P, EXP_COLS):
                    v = lot % 2
                    if lot >= 2:
                        pool.wait_ge(agg_pe, (lot - 1) * EXP_COLS // CHUNK)
                    pool.dma_start(experts[v][0:EXPERTS, :],
                                   mlp[m]["experts"][:, at:at + EXP_COLS]).then_inc(experts_loaded[v], 16)
                    pool.dma_start(experts[v][EXPERTS:EXPERTS + 1, :],
                                   eye.rearrange("(a i) o -> a (i o)", a=1)[:, at:at + EXP_COLS]
                                   ).then_inc(experts_loaded[v], 16)
                    lot += 1

            def middle(stage, j):
                pool.wait_ge(half_ready, stage + 1)
                if not (isinstance(stage, int) and stage < 2):
                    pool.wait_ge(y_ready, stage - 1)
                h1, h2 = half[:, j % 2, 0, :], half[:, j % 2, 1, :]
                pool.tensor_tensor(mid[:, j % 2, 0, :], h1, h2, ALU.add).then_inc(mid_ready, 1)
                pool.tensor_tensor(mid[:, j % 2, 1, :], h1, h2, ALU.subtract).then_inc(mid_ready, 1)

            def step(i):
                if is_front(i):
                    for j in range(PH):
                        middle(stage0(i, j), j)
                if is_back(i):
                    for j in range(PH):
                        middle(stage2(i - 1, j), j)

            pipeline(pool, step)

        PAR_LOADS = 16 * (2 + 2 * 7 + 3)

        @block.tensor
        def _(pe):
            pe.wait_ge(par_loaded, PAR_LOADS)
            pe.wait_ge(filled, 1)
            for m in range(2):
                pe.matmul(psum[:, m, 0, 0:B], par[m]["w0"], emb_sb, start=True, stop=True).then_inc(mlp_pe, 1)
            for m in range(2):
                pe.wait_ge(mlp_act, 1 + m)
                pe.matmul(psum[:, m, 1, 0:B], par[m]["w1"], hid[m]["h"], start=True, stop=True).then_inc(mlp_pe, 1)
            for m in range(2):
                pe.wait_ge(mlp_act, 3 + m)
                pe.matmul(psum[:, m, 2, 0:EXPERTS], hid[m]["h1"], par[m]["w2"], start=True, stop=False)
                pe.matmul(psum[:, m, 2, 0:EXPERTS], ones[0:1, 0:B], par[m]["b2"][0:1, :], start=False,
                          stop=True).then_inc(mlp_pe, 1)
            for m in range(2):
                pe.wait_ge(mlp_dve, 1 + m)
                pe.transpose(psum[0:EXPERTS, m, 3, 0:B], hid[m]["att"], eye_sb).then_inc(mlp_pe, 1)
            for v in range(2):
                pe.matmul(psum[:, v, 0, 0:B], ctx_sb[v], emb_sb, start=True, stop=True).then_inc(bias_pe, 1)
            pe.wait_ge(mlp_dve, 4)
            pe.matmul(psum[:, 0, 2, 0:B], par[1]["bias_k"][0:EXPERTS, :], hid[1]["att_t"][0:EXPERTS, :],
                      start=True, stop=True).then_inc(bias_pe, 1)
            for j in range(PH):
                for g in range(GROUPS):
                    mm = pe.matmul(psum[CG * j:CG * (j + 1), 1, 2, B * g:B * (g + 1)],
                                   par[0]["bias_k"][0:EXPERTS, CG * g:CG * (g + 1)],
                                   hid[0]["att_t"][0:EXPERTS, :], start=True, stop=True)
            mm.then_inc(bias_pe, 1)
            pe.wait_ge(bias_ready, 4)
            chunk = 0
            for m in range(2):
                for at in range(0, P * P, EXP_COLS):
                    lot = m * (P * P // EXP_COLS) + at // EXP_COLS
                    pe.wait_ge(experts_loaded[lot % 2], 32 * (lot // 2 + 1))
                    for c in range(0, EXP_COLS, CHUNK):
                        if chunk >= 2:
                            pe.wait_ge(agg_act, chunk - 1)
                            pe.wait_ge(agg_dve, chunk - 1)
                        for k in range(4):
                            mm = pe.matmul(psum[:, chunk % 2, k, :], hid[m]["att_t"][0:EXPERTS + 1, :],
                                           experts[lot % 2][0:EXPERTS + 1, c + k * BANK:c + (k + 1) * BANK],
                                           start=True, stop=True)
                        mm.then_inc(agg_pe, 1)
                        chunk += 1
            pe.wait_ge(agg_act, CHUNKS)
            pe.wait_ge(agg_dve, CHUNKS)
            pe.wait_ge(wino_ready, 2)

            def conv(v, j, free):
                for pos, kind in enumerate(KIND_ORDER):
                    free(pos)
                    for g in range(GROUPS):
                        mm = pe.matmul(psum[CG * g:CG * (g + 1), j % 2, kind, :], wino[v][:, kind, g, j, :],
                                       dif[v][:, kind, g, :, :].rearrange("p b r -> p (b r)"),
                                       start=True, stop=True)
                    mm.then_inc(kind_done, 1)

            def mix1(i, b):
                for g in range(GROUPS):
                    for j in range(PH):
                        mm = pe.matmul(psum[CG * j:CG * (j + 1), b, g, :], mixw[0][:, b, CG * g:CG * (g + 1)],
                                       y[0][:, j, b, :], start=True, stop=True)
                    mm.then_inc(mix1_done, 1)

            def mix3(n, b):
                for j in range(PH):
                    mm = pe.matmul(psum[:, b, j, :], mixw[1][:, b, :], y[1][:, j, b, :], start=True, stop=True)
                mm.then_inc(mix3_done, 1)

            def step(i):
                first = isinstance(i, int) and i == 0
                second = isinstance(i, int) and i == 1

                def conv_free(stage):
                    def free(pos):
                        if pos == 0:
                            pe.wait_ge(half_ready, stage - 1)
                        if pos == 2:
                            pe.wait_ge(y_ready, stage - 1)
                    return free

                if is_front(i):
                    for j in range(PH):
                        def free(pos, j=j):
                            if j == 0:
                                pe.wait_ge(dif0_ready, 4 * i + pos + 1)
                            if j < 2 and pos == 0 and not first:
                                if second:
                                    pe.wait_ge(xph1_ready, GROUPS * (j + 1))
                                else:
                                    pe.wait_ge(out_ready, PB * (i - 2) + j + 1)
                            if j >= 2:
                                conv_free(stage0(i, j))(pos)
                        conv(0, j, free)
                if is_back(i):
                    for j in range(PH):
                        def free(pos, j=j):
                            if j == 0:
                                pe.wait_ge(dif2_ready, 4 * (i - 1) + pos + 1)
                            if j >= 2:
                                conv_free(stage2(i - 1, j))(pos)
                            elif is_front(i):
                                conv_free(stage2(i - 1, j))(pos)
                            elif pos == 0:
                                pe.wait_ge(out_ready, PB * (i - 2) + j + 1)
                        conv(1, j, free)
                if is_front(i):
                    pe.wait_ge(y_ready, stage0(i, PH - 1) + 1)
                    pe.wait_ge(mix1_loaded, 16 * PB * (i + 1))
                    for b in range(PB):
                        if is_back(i):
                            pe.wait_ge(y_ready, stage2(i - 1, 2 + b) + 1)
                        mix1(i, b)
                if is_back(i):
                    pe.wait_ge(y_ready, stage2(i - 1, PH - 1) + 1)
                    pe.wait_ge(mix3_loaded, 16 * PB * i)
                    for b in range(PB):
                        if is_front(i):
                            pe.wait_ge(xph1_ready, PB * GROUPS * i + GROUPS * (b + 1))
                        mix3(i - 1, b)

            pipeline(pe, step)

        @block.scalar
        def _(act):
            act.wait_ge(par_loaded, PAR_LOADS)
            for layer, (bias, hout) in enumerate((("b0", "h"), ("b1", "h1"))):
                for m in range(2):
                    act.wait_ge(mlp_pe, 2 * layer + m + 1)
                    nc.scalar.activation(hid[m][hout], psum[:, m, layer, 0:B], ACT.Gelu,
                                         bias=par[m][bias]).then_inc(mlp_act, 1)
            for m in range(2):
                act.wait_ge(max_ready, 1 + m)
                nc.scalar.activation(hid[m]["exp"], psum[:, m, 2, 0:EXPERTS], ACT.Exp, bias=hid[m]["nmax"],
                                     accum_out=hid[m]["sum"]).then_inc(mlp_act, 1)
            for chunk in range(CHUNKS):
                act.wait_ge(agg_pe, chunk + 1)
                if chunk >= 2:
                    act.wait_ge(agg_stored[chunk % 2], 16 * (chunk // 2))
                nc.scalar.copy(stage_out[:, chunk % 2, 0:2 * BANK].rearrange("p (k n) -> p k n", k=2),
                               psum[:, chunk % 2, 0:2, :]).then_inc(agg_act, 1)

            def copy_lot(n, lot):
                if lot == 0:
                    act.wait_ge(x_loaded, 16 * PB * (n + 1))
                    if not (isinstance(n, int) and n == 0):
                        act.wait_ge(dif0_ready, 4 * n)
                size = len(ACT_COPIES) // PH
                for p, g in ACT_COPIES[lot * size:(lot + 1) * size]:
                    dst, src = phase_copy(p, g)
                    c = nc.scalar.copy(dst, src)
                if lot == PH - 1:
                    c.then_inc(phased_act, 1)

            def halves(v, stage, j):
                act.wait_ge(kind_done, 4 * stage + 1)
                if not (isinstance(stage, int) and stage < 2):
                    act.wait_ge(mid_ready, 2 * (stage - 1))
                for b in range(PB):
                    nc.scalar.activation(half[:, j % 2, 0, b * R:(b + 1) * R], psum[:, j % 2, 1, b * R:(b + 1) * R],
                                         ACT.Identity, bias=bias_now[:, v, b, CONV_BIAS[v]:CONV_BIAS[v] + 1])
                act.wait_ge(kind_done, 4 * stage + 2)
                nc.scalar.copy(half[:, j % 2, 1, :], psum[:, j % 2, 2, :]).then_inc(half_ready, 1)

            act.wait_ge(bias_ready, 4)
            act.wait_ge(filled, 2)
            for lot in range(PH):
                copy_lot(0, lot)

            def pick_biases(i):
                if is_back(i):
                    act.wait_ge(xph1_ready, PB * GROUPS * i)
                if not (isinstance(i, int) and i <= 1):
                    act.wait_ge(out_ready, PB * (i - 1))
                act.wait_ge(bias_ready, 4)
                for back in range(2):
                    if is_back(i) if back else is_front(i):
                        nc.scalar.copy(bias_now[:, back], bias_table[:, bass.ds(PB * (i - back), PB), :]
                                       ).then_inc(bias_picked, 1)
                act.wait_ge(bias_picked, 1 if isinstance(i, int) and i == 0 else
                            2 * i + (0 if isinstance(i, int) and i == PAIRS else 1))

            def step(i):
                pick_biases(i)
                if is_front(i):
                    for j in range(PH):
                        halves(0, stage0(i, j), j)
                        if has(i, 1):
                            copy_lot(i + 1, j)
                if is_back(i):
                    for j in range(PH):
                        halves(1, stage2(i - 1, j), j)
                if is_front(i):
                    if is_back(i):
                        act.wait_ge(dif2_ready, 4 * i)
                    for b in range(PB):
                        for g in range(GROUPS):
                            act.wait_ge(mix1_done, PB * GROUPS * i + GROUPS * b + g + 1)
                            nc.scalar.activation(xph[1][:, g, b, 1:S + 1], psum[:, b, g, :], ACT.Identity,
                                                 bias=bias_now[:, 0, b, MIX1_BIAS + g:MIX1_BIAS + g + 1]
                                                 ).then_inc(xph1_ready, 1)
                if is_back(i):
                    for b in range(PB):
                        act.wait_ge(mix3_done, PB * (i - 1) + b + 1)
                        if not (isinstance(i, int) and i == 1):
                            act.wait_ge(out_stored[b], 16 * (i - 1))
                        nc.scalar.activation(outb[:, b, :].rearrange("p (s j) -> p j s", j=PH), psum[:, b, :, :],
                                             ACT.Identity, bias=bias_now[:, 1, b, MIX3_BIAS:MIX3_BIAS + 1]
                                             ).then_inc(out_ready, 1)

            pipeline(act, step)

        @block.vector
        def _(dve):
            chain = [0]

            def link(ins):
                chain[0] += 1
                ins.then_inc(wino_step, 1)
                dve.wait_ge(wino_step, chain[0])

            for v in range(2):
                nc.vector.memset(blocks[v].rearrange("p m g j o -> p (m g j o)"), 0.0).then_inc(taps_cleared, 1)
            nc.vector.memset(ones, 1.0)
            for m in range(2):
                last = nc.vector.memset(hid[m]["att_t"][0:EXPERTS + 1, :], 1.0)
            last.then_inc(filled, 1)
            for v in range(2):
                edge = xph[v][:].rearrange("p g b s -> p (g b) s")
                nc.vector.memset(edge[:, :, 0:1], 0.0)
                last = nc.vector.memset(edge[:, :, S + 1:S + 2], 0.0)
            last.then_inc(filled, 1)
            dve.wait_ge(filled, 2)
            for m in range(2):
                dve.wait_ge(mlp_pe, 5 + m)
                nc.vector.tensor_reduce(hid[m]["nmax"], psum[:, m, 2, 0:EXPERTS], AX.X, ALU.max,
                                        negate=True).then_inc(max_ready, 1)
            for m in range(2):
                dve.wait_ge(mlp_act, 5 + m)
                link(nc.vector.reciprocal(hid[m]["inv"], hid[m]["sum"]))
                nc.vector.tensor_scalar(hid[m]["att"], hid[m]["exp"], hid[m]["inv"], None,
                                        ALU.mult).then_inc(mlp_dve, 1)
            for m in range(2):
                dve.wait_ge(mlp_pe, 7 + m)
                nc.vector.tensor_copy(hid[m]["att_t"][0:EXPERTS, :],
                                      psum[0:EXPERTS, m, 3, 0:B]).then_inc(mlp_dve, 1)
            for v in range(2):
                dve.wait_ge(bias_pe, v + 1)
                nc.vector.tensor_scalar(bias_table[:, :, CONV_BIAS[v]], psum[:, v, 0, 0:B], fside_sb, None,
                                        ALU.add).then_inc(bias_ready, 1)
            dve.wait_ge(bias_pe, 3)
            nc.vector.tensor_copy(bias_table[:, :, MIX3_BIAS], psum[:, 0, 2, 0:B]).then_inc(bias_ready, 1)
            dve.wait_ge(bias_pe, 4)
            nc.vector.tensor_copy(
                bias_table[:, :, MIX1_BIAS:MIX1_BIAS + GROUPS].rearrange("p b g -> p g b"),
                psum[:, 1, 2, :].rearrange("p (g b) -> p g b", g=GROUPS)).then_inc(bias_ready, 1)
            for chunk in range(CHUNKS):
                dve.wait_ge(agg_pe, chunk + 1)
                if chunk >= 2:
                    dve.wait_ge(agg_stored[chunk % 2], 16 * (chunk // 2))
                nc.vector.tensor_copy(stage_out[:, chunk % 2, 2 * BANK:4 * BANK].rearrange("p (k n) -> p k n", k=2),
                                      psum[:, chunk % 2, 2:4, :]).then_inc(agg_dve, 1)
            taps_each = sum(0 <= PH * (m - 1) + p - j + HALO < TAPS
                            for p in range(PH) for j in range(PH) for m in range(3))
            for v in range(2):
                dve.wait_ge(taps_loaded, 16 * taps_each * 2)
                before, here, after = (blocks[v][:, m].rearrange("p g j o -> p g (j o)") for m in range(3))
                w = [wino[v][:, k].rearrange("p g j o -> p g (j o)") for k in range(4)]
                for g in range(GROUPS):
                    link(nc.vector.tensor_tensor(here[:, g], here[:, g], eye_sb, ALU.add))
                link(nc.vector.tensor_copy(w[0], before))
                link(nc.vector.tensor_copy(w[3], after))
                link(nc.vector.tensor_tensor(before, before, after, ALU.add))
                link(nc.vector.tensor_tensor(w[1], before, here, ALU.add))
                link(nc.vector.tensor_tensor(w[2], before, here, ALU.subtract))
                link(nc.vector.tensor_scalar(w[1], w[1], 0.5, None, ALU.mult))
                nc.vector.tensor_scalar(w[2], w[2], 0.5, None, ALU.mult).then_inc(wino_ready, 1)

            def copy_in(n):
                dve.wait_ge(x_loaded, 16 * PB * (n + 1))
                for p, g in DVE_COPIES:
                    dst, src = phase_copy(p, g)
                    c = nc.vector.tensor_copy(dst, src)
                c.then_inc(phased_dve, 1)

            def sums(v, kind, ready):
                a = xph[v][:].rearrange("p g b s -> p (g b) s")
                d = [a[:, :, q:q + 2 * R - 1:2] for q in range(4)]
                in0, in1, op = {0: (d[0], d[2], ALU.subtract), 1: (d[1], d[2], ALU.add),
                                2: (d[2], d[1], ALU.subtract), 3: (d[1], d[3], ALU.subtract)}[kind]
                nc.vector.tensor_tensor(dif[v][:, kind].rearrange("p g b r -> p (g b) r"), in0, in1,
                                        op).then_inc(ready, 1)

            def outputs(v, stage, j):
                o = y[v][:, j]
                dve.wait_ge(kind_done, 4 * stage + 3)
                dve.wait_ge(mid_ready, 2 * stage + 1)
                nc.vector.tensor_tensor(o[:, :, 0:S:2], psum[:, j % 2, 0, :].rearrange("p (b r) -> p b r", b=PB),
                                        mid[:, j % 2, 0, :].rearrange("p (b r) -> p b r", b=PB), ALU.add)
                dve.wait_ge(kind_done, 4 * stage + 4)
                dve.wait_ge(mid_ready, 2 * stage + 2)
                nc.vector.tensor_tensor(o[:, :, 1:S:2], mid[:, j % 2, 1, :].rearrange("p (b r) -> p b r", b=PB),
                                        psum[:, j % 2, 3, :].rearrange("p (b r) -> p b r", b=PB),
                                        ALU.subtract).then_inc(y_ready, 1)

            copy_in(0)
            dve.wait_ge(phased_act, 1)
            dve.wait_ge(phased_dve, 1)
            dve.wait_ge(agg_pe, CHUNKS)
            for kind in KIND_ORDER:
                sums(0, kind, dif0_ready)
            dve.wait_ge(dif0_ready, 4)
            copy_in(1)

            def step(i):
                if is_front(i):
                    for j in range(PH):
                        if is_back(i):
                            if j == 0:
                                dve.wait_ge(xph1_ready, PB * GROUPS * i)
                            sums(1, KIND_ORDER[j], dif2_ready)
                        if j == 0 and is_back(i):
                            dve.wait_ge(mix1_done, PB * GROUPS * i)
                        outputs(0, stage0(i, j), j)
                else:
                    dve.wait_ge(xph1_ready, PB * GROUPS * i)
                    for kind in KIND_ORDER:
                        sums(1, kind, dif2_ready)
                for j in range(PH):
                    if has(i, 1):
                        if j == 0:
                            dve.wait_ge(phased_act, i + 2)
                            dve.wait_ge(phased_dve, i + 2)
                            dve.wait_ge(kind_done, 4 * stage0(i, PH - 1) + 4)
                        sums(0, KIND_ORDER[j], dif0_ready)
                    if is_back(i):
                        if j == 0 and not (isinstance(i, int) and i == 1):
                            dve.wait_ge(mix3_done, PB * (i - 1))
                        outputs(1, stage2(i - 1, j), j)
                if has(i, 2):
                    dve.wait_ge(dif0_ready, 4 * (i + 2))
                    copy_in(i + 2)

            pipeline(dve, step)


def kernel(x, cond_128, fside_S_0, L0_cond_weight, L0_cond_c_weight, L1_cond_W0, L1_cond_b0, L1_cond_W1, L1_cond_b1,
           L1_cond_W2, L1_cond_b2, L1_cond_weight, L1_cond_bias_k, L2_cond_weight, L2_cond_c_weight, L3_cond_W0,
           L3_cond_b0, L3_cond_W1, L3_cond_b1, L3_cond_W2, L3_cond_b2, L3_cond_weight, L3_cond_bias_k):
    import numpy as np
    import concourse.bacc as bacc
    from concourse.bass_utils import run_bass_kernel_spmd

    nc = bacc.Bacc("TRN2", target_bir_lowering=False, num_devices=1)
    arrays = {}

    def give(name, a):
        a = np.ascontiguousarray(a)
        arrays[name] = a
        return nc.dram_tensor(name, a.shape, mybir.dt.from_np(a.dtype), kind="ExternalInput").ap()

    def taps(w):
        w = np.asarray(w)
        o, c, k = w.shape
        return w.reshape(o // c, c, c, k).transpose(3, 2, 0, 1)

    def experts(w):
        w = np.asarray(w)
        return w[..., 0].transpose(0, 2, 1).reshape(w.shape[0], -1)

    def col(a):
        return np.asarray(a).reshape(-1, 1)

    def row(a):
        return np.asarray(a).reshape(1, -1)

    x = np.asarray(x)
    args = {
        "x": give("x", x),
        "emb_t": give("emb_t", np.asarray(cond_128).T),
        "eye": give("eye", np.eye(x.shape[1], dtype=np.float32)),
        "fside": give("fside", col(fside_S_0)),
        "conv_w": [give("conv_w0", taps(L0_cond_weight)), give("conv_w2", taps(L2_cond_weight))],
        "ctx_w": [give("ctx_w0", np.asarray(L0_cond_c_weight).T), give("ctx_w2", np.asarray(L2_cond_c_weight).T)],
        "mlp": [
            {"w0": give("w0_1", L1_cond_W0), "b0": give("b0_1", col(L1_cond_b0)), "w1": give("w1_1", L1_cond_W1),
             "b1": give("b1_1", col(L1_cond_b1)), "w2": give("w2_1", L1_cond_W2), "b2": give("b2_1", row(L1_cond_b2)),
             "experts": give("experts_1", experts(L1_cond_weight)), "bias_k": give("bias_k_1", L1_cond_bias_k)},
            {"w0": give("w0_3", L3_cond_W0), "b0": give("b0_3", col(L3_cond_b0)), "w1": give("w1_3", L3_cond_W1),
             "b1": give("b1_3", col(L3_cond_b1)), "w2": give("w2_3", L3_cond_W2), "b2": give("b2_3", row(L3_cond_b2)),
             "experts": give("experts_3", experts(L3_cond_weight)), "bias_k": give("bias_k_3", L3_cond_bias_k)},
        ],
        "out": nc.dram_tensor("out", x.shape, F32, kind="ExternalOutput").ap(),
    }
    conditioned_layers(nc, **args)
    r = run_bass_kernel_spmd(nc, [arrays], core_ids=[0])
    return r.results[0]["out"]
```

```python
from contextlib import ExitStack

import concourse.bass as bass
from concourse import mybir

F32 = mybir.dt.float32
BF16 = mybir.dt.bfloat16
ALU = mybir.AluOpType
ACT = mybir.ActivationFunctionType
AX = mybir.AxisListType

P = 128
GROUPS = 4
CG = P // GROUPS
PH = 4
HALVES = 2
BANK = 512
PB = 2
CONV_BIAS, MIX1_BIAS, MIX3_BIAS, BIASES = (0, 1), 2, 6, 7
KIND_ORDER = (1, 2, 0, 3)


def conditioned_layers(nc, x, wide, bias_k, b2, experts, conv_w, out):
    B, C, L = x.shape
    S = L // PH
    R = S // 2
    TAPS = conv_w[0].shape[0]
    HALO = TAPS // 2
    PAIRS = B // PB
    EXPERTS = bias_k.shape[0]
    PARTS = 3
    ROWS = PARTS * PARTS * EXPERTS + 1
    SPLIT = EXPERTS * P * P // P
    CHUNK = 4 * BANK
    CHUNKS = P * P // CHUNK
    assert C == P and B == P and S == BANK and PB * R == BANK and TAPS == 2 * PH + 1 and PAIRS > 4

    mix_dram = [nc.dram_tensor(f"mix_dram{m}", (B, P * P), F32).ap() for m in range(2)]

    parts_dram = [nc.dram_tensor(f"parts_dram{m}", (PARTS * EXPERTS + 1, P * P), BF16).ap() for m in range(2)]

    with ExitStack() as ctx:
        def sb(name, shape, dtype=F32):
            return ctx.enter_context(nc.sbuf_tensor(name, shape, dtype))

        def sem(name):
            return ctx.enter_context(nc.semaphore(name))

        xin = sb("xin", [P, PB, L])
        xph = [sb(f"xph{v}", [P, GROUPS, PB, S + 2]) for v in range(2)]
        dif = [sb(f"dif{v}", [P, 4, GROUPS, PB, R]) for v in range(2)]
        y = [sb(f"y{v}", [P, PH, PB, S]) for v in range(2)]
        outb = sb("outb", [P, PB, L])
        half = sb("half", [P, 2, BANK])
        mid = sb("mid", [P, 2, 2, BANK])
        rows = sb("rows", [ROWS, 2, CHUNK], BF16)
        wino = [sb(f"wino{v}", [P, 4, PH, GROUPS, CG]) for v in range(2)]
        mixw = [sb(f"mixw{m}", [P, PB, P]) for m in range(2)]
        bias_table = sb("bias_table", [P, B, BIASES])
        bias_now = sb("bias_now", [P, 2, PB, BIASES])
        psum = ctx.enter_context(nc.psum_tensor("psum", [P, HALVES, 4, BANK], F32))

        blocks = [y[v][:].rearrange("p j b s -> p (j b s)")[:, 0:3 * BANK].rearrange(
            "p (m j g o) -> p m j g o", m=3, g=GROUPS, j=PH) for v in range(2)]
        room = [y[v][:].rearrange("p j b s -> p (j b s)")[:, 3 * BANK:] for v in range(2)]
        flat = xph[1][:].rearrange("p g b s -> p (g b s)")
        part = [[flat[:, (2 * q + m) * SPLIT // 2:(2 * q + m + 1) * SPLIT // 2].bitcast(BF16) for m in range(2)]
                for q in range(PARTS)]
        rest = [mid[:, m, :, :].rearrange("p a n -> p (a n)") for m in range(2)]

        used = [0, 0]

        def carve(v, cols):
            used[v] += cols
            return room[v][:, used[v] - cols:used[v]]

        ones = carve(0, P)
        wide_sb = carve(1, wide.shape[1])
        wide_at = [0]

        def field(cols):
            wide_at[0] += cols
            return wide_sb[:, wide_at[0] - cols:wide_at[0]]

        emb_sb, eye_sb, eye_down, fside_sb = field(B), field(P), field(P), field(1)
        ctx_sb = [field(P) for _ in range(2)]
        par = [{"w0": field(P), "w1": field(P), "w2": field(EXPERTS), "b0": field(1), "b1": field(1)}
               for _ in range(2)]
        assert wide_at[0] == wide.shape[1]
        bias_k_sb = carve(0, 2 * P)[0:EXPERTS, :].rearrange("k (m o) -> k m o", m=2)
        b2_sb = carve(0, 2 * EXPERTS)[0:1, :].rearrange("a (m k) -> a m k", m=2)
        eye16 = carve(1, P // 2).bitcast(BF16)
        hid = [{"h": carve(0, P), "h1": carve(0, P), "nmax": carve(0, 1), "exp": carve(0, EXPERTS),
                "sum": carve(0, 1), "inv": carve(0, 1), "att": carve(0, EXPERTS), "att_t": carve(0, P),
                "part": [carve(0, EXPERTS // 2).bitcast(BF16) for _ in range(PARTS)],
                "rest": [carve(0, EXPERTS) for _ in range(PARTS - 1)], "rows": carve(0, ROWS),
                "rows_t": sb(f"att_rows_t{m}", [ROWS, P], BF16)} for m in range(2)]

        par_loaded = sem("par_loaded")
        taps_loaded = [sem(f"taps_loaded{v}") for v in range(2)]
        taps_cleared = sem("taps_cleared")
        experts_loaded = [sem(f"experts_loaded{m}") for m in range(2)]
        parts_ready = sem("parts_ready")
        parts_stored = [sem(f"parts_stored{m}") for m in range(2)]
        rows_loaded = [sem(f"rows_loaded{v}") for v in range(2)]
        wino_step = [sem(f"wino_step{v}") for v in range(2)]
        wino_ready = [sem(f"wino_ready{v}") for v in range(2)]
        dve_step = sem("dve_step")
        filled = sem("filled")
        mlp_pe = sem("mlp_pe")
        mlp_act = sem("mlp_act")
        max_ready = sem("max_ready")
        mlp_dve = sem("mlp_dve")
        bias_pe = sem("bias_pe")
        bias_ready = sem("bias_ready")
        agg_pe = sem("agg_pe")
        agg_act = sem("agg_act")
        agg_stored = [sem(f"agg_stored{v}") for v in range(2)]

        bias_picked = sem("bias_picked")
        x_loaded = sem("x_loaded")
        phased = sem("phased")
        dif0_ready = sem("dif0_ready")
        dif2_ready = sem("dif2_ready")
        kind_done = sem("kind_done")
        half_ready = sem("half_ready")
        mid_ready = sem("mid_ready")
        y_ready = sem("y_ready")
        mix1_loaded = sem("mix1_loaded")
        mix3_loaded = sem("mix3_loaded")
        mix1_done = sem("mix1_done")
        xph1_ready = sem("xph1_ready")
        mix3_done = sem("mix3_done")
        out_ready = sem("out_ready")
        out_stored = [sem(f"out_stored{b}") for b in range(PB)]

        def stage0(i, j):
            return j if isinstance(i, int) and i == 0 else 8 * i - 4 + j

        def stage2(n, j):
            return 8 * n + 8 + j - (4 if isinstance(n, int) and n == PAIRS - 1 else 0)

        def pipeline(eng, step):
            step(0)
            step(1)
            with eng.Fori(2, PAIRS - 2) as i:
                step(i)
            step(PAIRS - 2)
            step(PAIRS - 1)
            step(PAIRS)

        def is_front(i):
            return not (isinstance(i, int) and i >= PAIRS)

        def is_back(i):
            return not (isinstance(i, int) and i < 1)

        def has(i, ahead):
            return not (isinstance(i, int) and i + ahead >= PAIRS)

        COPIES = [(p, g) for p in range(PH) for g in range(GROUPS)]
        LOTS = 2 * PH

        def phase_copy(p, g):
            dst = xph[0][CG * p:CG * (p + 1), g, :, 1:S + 1]
            src = xin[CG * g:CG * (g + 1), :, p:p + PH * (S - 1) + 1:PH]
            return dst, src

        PAR_LOADS = 16 * 3

        block = ctx.enter_context(nc.Block())

        @block.sync
        def _(sp):
            for v in range(2):
                sp.wait_ge(taps_cleared, v + 1)
                line = blocks[v].rearrange("p m j g o -> p (m j) g o")
                for p in range(PH):
                    sp.dma_start(line[CG * p:CG * (p + 1), PH - 1 - p:PH - 1 - p + TAPS],
                                 conv_w[v].rearrange("k c g o -> c k g o")).then_inc(taps_loaded[v], 16)
                if v == 0:
                    for b in range(PB):
                        sp.dma_start(xin[:, b, :], x[b]).then_inc(x_loaded, 16)

            def load_x(n):
                if not (isinstance(n, int) and n == 0):
                    sp.wait_ge(phased, n + 1)
                for b in range(PB):
                    sp.dma_start(xin[:, b, :], x[PB * n + b]).then_inc(x_loaded, 16)

            def store_parts(m):
                sp.wait_ge(parts_ready, m + 1)
                for q in range(PARTS):
                    sp.dma_start(parts_dram[m][q * EXPERTS:(q + 1) * EXPERTS, :].rearrange(
                        "k (q c) -> (k q) c", c=SPLIT), part[q][m]).then_inc(parts_stored[m], 16)
                sp.dma_start(parts_dram[m][PARTS * EXPERTS, :].rearrange("(i o) -> i o", i=P),
                             eye16).then_inc(parts_stored[m], 16)
                sp.wait_ge(parts_stored[m], 16 * (PARTS + 1))
                for c in range(2):
                    load_rows(m, c)

            def load_rows(m, c):
                chunk = m * CHUNKS + c
                if chunk >= 2:
                    sp.wait_ge(agg_pe, 2 * (chunk - 1))
                for qa in range(PARTS):
                    n = PARTS * EXPERTS + (1 if qa == PARTS - 1 else 0)
                    sp.dma_start(rows[PARTS * EXPERTS * qa:PARTS * EXPERTS * qa + n, c % 2, :],
                                 parts_dram[m][0:n, c * CHUNK:(c + 1) * CHUNK]).then_inc(rows_loaded[c % 2], 16)

            def store_agg(m):
                for c in range(CHUNKS):
                    chunk = m * CHUNKS + c
                    sp.wait_ge(agg_act, 2 * (chunk + 1))
                    sp.dma_start(mix_dram[m][:, c * CHUNK:(c + 1) * CHUNK], outb[:, c % 2, :]
                                 ).then_inc(agg_stored[c % 2], 16)
                    if c + 2 < CHUNKS:
                        load_rows(m, c + 2)
                for v in range(2):
                    sp.wait_ge(agg_stored[v], 16 * CHUNKS * (m + 1) // 2)

            def load_mix(m, n):
                if not (isinstance(n, int) and n == 0):
                    if m == 0:
                        sp.wait_ge(mix1_done, PB * GROUPS * n)
                    else:
                        sp.wait_ge(mix3_done, PB * n)
                for b in range(PB):
                    src = mix_dram[m].rearrange("b (i o) -> b i o", i=P)
                    sp.dma_start(mixw[m][:, b, :], src[PB * n + b]).then_inc((mix1_loaded, mix3_loaded)[m], 16)

            store_parts(0)
            store_agg(0)
            load_mix(0, 0)
            load_x(1)
            store_parts(1)

            def step(i):
                if isinstance(i, int) and i == 1:
                    store_agg(1)
                    load_mix(1, 0)
                if has(i, 2):
                    load_x(i + 2)
                if has(i, 1):
                    load_mix(0, i + 1)
                if is_back(i):
                    for b in range(PB):
                        sp.wait_ge(out_ready, PB * (i - 1) + b + 1)
                        sp.dma_start(out[PB * (i - 1) + b], outb[:, b, :]).then_inc(out_stored[b], 16)
                    if has(i, 0):
                        load_mix(1, i)

            pipeline(sp, step)
            for b in range(PB):
                sp.wait_ge(out_stored[b], 16 * PAIRS)

        def weights_of(v, eng, done):
            count = 0

            def link(ins):
                nonlocal count
                count += 1
                ins.then_inc(done, 1)
                eng.wait_ge(done, count)

            eng.wait_ge(par_loaded, PAR_LOADS)
            eng.wait_ge(taps_loaded[v], 16 * PH)
            before, here, after = (blocks[v][:, m].rearrange("p j g o -> p (j g o)") for m in range(3))
            w = [wino[v][:, k].rearrange("p j g o -> p (j g o)") for k in range(4)]
            for g in range(GROUPS):
                link(eng.tensor_tensor(blocks[v][:, 1, :, g, :], blocks[v][:, 1, :, g, :],
                                       eye_down.rearrange("p (j o) -> p j o", j=PH), ALU.add))
            link(eng.tensor_copy(w[0], before))
            link(eng.tensor_copy(w[3], after))
            link(eng.tensor_tensor(before, before, after, ALU.add))
            link(eng.tensor_tensor(w[1], before, here, ALU.add))
            link(eng.tensor_tensor(w[2], before, here, ALU.subtract))
            link(eng.tensor_scalar(w[1], w[1], 0.5, None, ALU.mult))
            eng.tensor_scalar(w[2], w[2], 0.5, None, ALU.mult).then_inc(wino_ready[v], 1)

        @block.gpsimd
        def _(pool):
            for v in range(2):
                pool.memset(blocks[v].rearrange("p m j g o -> p (m j g o)"), 0.0).then_inc(taps_cleared, 1)
            for v in range(2):
                weights_of(v, pool, wino_step[v])

        @block.tensor
        def _(pe):
            pe.wait_ge(par_loaded, PAR_LOADS)
            pe.wait_ge(filled, 1)
            for m in range(2):
                pe.matmul(psum[:, m, 0, 0:B], par[m]["w0"], emb_sb, start=True, stop=True).then_inc(mlp_pe, 1)
            for m in range(2):
                pe.wait_ge(mlp_act, 1 + m)
                pe.matmul(psum[:, m, 1, 0:B], par[m]["w1"], hid[m]["h"], start=True, stop=True).then_inc(mlp_pe, 1)
            for m in range(2):
                pe.wait_ge(mlp_act, 3 + m)
                pe.matmul(psum[:, m, 2, 0:EXPERTS], hid[m]["h1"], par[m]["w2"], start=True, stop=False)
                pe.matmul(psum[:, m, 2, 0:EXPERTS], ones[0:1, 0:B], b2_sb[:, m, :], start=False,
                          stop=True).then_inc(mlp_pe, 1)
            for m in range(2):
                pe.wait_ge(mlp_dve, 1 + m)
                pe.transpose(psum[0:EXPERTS, m, 3, 0:B], hid[m]["att"], eye_sb).then_inc(mlp_pe, 1)
                pe.transpose(psum[0:ROWS, m, 3, B:2 * B], hid[m]["rows"], eye_sb).then_inc(mlp_pe, 1)
            for v in range(2):
                pe.matmul(psum[:, v, 0, 0:B], ctx_sb[v], emb_sb, start=True, stop=True).then_inc(bias_pe, 1)
            pe.wait_ge(mlp_dve, 6)
            pe.matmul(psum[:, 0, 2, 0:B], bias_k_sb[:, 1, :], hid[1]["att_t"][0:EXPERTS, :],
                      start=True, stop=True).then_inc(bias_pe, 1)
            for j in range(PH):
                for g in range(GROUPS):
                    mm = pe.matmul(psum[CG * j:CG * (j + 1), 1, 2, B * g:B * (g + 1)],
                                   bias_k_sb[:, 0, CG * g:CG * (g + 1)],
                                   hid[0]["att_t"][0:EXPERTS, :], start=True, stop=True)
            mm.then_inc(bias_pe, 1)
            pe.wait_ge(bias_ready, 4)

            def aggregate(chunk):
                m, c = divmod(chunk, CHUNKS)
                pe.wait_ge(rows_loaded[c % 2], 16 * PARTS * (chunk // 2 + 1))
                for n, k in enumerate(KIND_ORDER):
                    mm = pe.matmul(psum[:, c % 2, k, :], hid[m]["rows_t"][:], rows[:, c % 2, k * BANK:(k + 1) * BANK],
                                   start=True, stop=True)
                    if n % 2:
                        mm.then_inc(agg_pe, 1)

            for c in range(CHUNKS):
                if c >= 2:
                    pe.wait_ge(agg_act, 2 * (c - 1))
                aggregate(c)
            pe.wait_ge(agg_act, 2 * CHUNKS)
            pe.wait_ge(wino_ready[0], 1)

            def conv(v, j, free):
                for pos, kind in enumerate(KIND_ORDER):
                    free(pos)
                    for g in range(GROUPS):
                        mm = pe.matmul(psum[CG * g:CG * (g + 1), j % 2, kind, :], wino[v][:, kind, PH - 1 - j, g, :],
                                       dif[v][:, kind, g, :, :].rearrange("p b r -> p (b r)"),
                                       start=True, stop=True)
                    mm.then_inc(kind_done, 1)

            def mix1(i, b):
                for g in range(GROUPS):
                    for j in range(PH):
                        mm = pe.matmul(psum[CG * j:CG * (j + 1), b, g, :], mixw[0][:, b, CG * g:CG * (g + 1)],
                                       y[0][:, j, b, :], start=True, stop=True)
                    mm.then_inc(mix1_done, 1)

            def mix3(n, b):
                for j in range(PH):
                    mm = pe.matmul(psum[:, b, j, :], mixw[1][:, b, :], y[1][:, j, b, :], start=True, stop=True)
                mm.then_inc(mix3_done, 1)

            def step(i):
                first = isinstance(i, int) and i == 0
                second = isinstance(i, int) and i == 1

                def chunk_before(stage, c, j):
                    if c < 2:
                        pe.wait_ge(xph1_ready, GROUPS * (j + 1))
                    else:
                        pe.wait_ge(half_ready, stage - 1)
                        pe.wait_ge(mid_ready, 2 * (stage - 1))
                        pe.wait_ge(y_ready, stage - 1)
                    aggregate(CHUNKS + c)

                def after_chunk(c, pos):
                    if pos % 2 == 0:
                        pe.wait_ge(agg_act, 2 * (CHUNKS + c) + pos // 2 + 1)

                def conv_free(stage):
                    def free(pos):
                        if pos == 0:
                            pe.wait_ge(half_ready, stage - 1)
                        if pos == 1:
                            pe.wait_ge(mid_ready, 2 * (stage - 1))
                        if pos == 2:
                            pe.wait_ge(y_ready, stage - 1)
                    return free

                if is_front(i):
                    for j in range(PH):
                        def free(pos, j=j):
                            if j == 0:
                                pe.wait_ge(dif0_ready, 4 * i + pos + 1)
                            if j < 2 and pos == 0 and not first:
                                if not second:
                                    pe.wait_ge(out_ready, PB * (i - 2) + j + 1)
                            if second:
                                after_chunk(j, pos)
                            elif j >= 2:
                                conv_free(stage0(i, j))(pos)
                        if second:
                            chunk_before(stage0(i, j), j, j)
                        conv(0, j, free)
                if is_back(i):
                    for j in range(PH):
                        def free(pos, j=j):
                            if j == 0:
                                pe.wait_ge(dif2_ready, 4 * (i - 1) + pos + 1)
                            if second:
                                after_chunk(PH + j, pos)
                            elif j >= 2:
                                conv_free(stage2(i - 1, j))(pos)
                            elif is_front(i):
                                conv_free(stage2(i - 1, j))(pos)
                            elif pos == 0:
                                pe.wait_ge(out_ready, PB * (i - 2) + j + 1)
                        if second:
                            chunk_before(stage2(0, j), PH + j, j)
                        conv(1, j, free)
                if is_front(i):
                    pe.wait_ge(y_ready, stage0(i, PH - 1) + 1)
                    pe.wait_ge(mix1_loaded, 16 * PB * (i + 1))
                    for b in range(PB):
                        if is_back(i):
                            pe.wait_ge(y_ready, stage2(i - 1, 2 + b) + 1)
                        mix1(i, b)
                    if not is_back(i):
                        pe.wait_ge(wino_ready[1], 1)
                if is_back(i):
                    pe.wait_ge(y_ready, stage2(i - 1, PH - 1) + 1)
                    pe.wait_ge(mix3_loaded, 16 * PB * i)
                    for b in range(PB):
                        if is_front(i):
                            pe.wait_ge(xph1_ready, PB * GROUPS * i + GROUPS * (b + 1))
                        mix3(i - 1, b)

            pipeline(pe, step)

        @block.scalar
        def _(act):
            act.dma_start(rest[0], experts[0].rearrange("k (q c) -> (k q) c", c=SPLIT)).then_inc(experts_loaded[0], 16)
            act.dma_start(wide_sb, wide).then_inc(par_loaded, 16)
            act.dma_start(bias_k_sb, bias_k).then_inc(par_loaded, 16)
            act.dma_start(b2_sb, b2).then_inc(par_loaded, 16)
            act.dma_start(rest[1], experts[1].rearrange("k (q c) -> (k q) c", c=SPLIT)).then_inc(experts_loaded[1], 16)
            act.wait_ge(par_loaded, PAR_LOADS)
            for layer, (bias, hout) in enumerate((("b0", "h"), ("b1", "h1"))):
                for m in range(2):
                    act.wait_ge(mlp_pe, 2 * layer + m + 1)
                    nc.scalar.activation(hid[m][hout], psum[:, m, layer, 0:B], ACT.Gelu,
                                         bias=par[m][bias]).then_inc(mlp_act, 1)
            for m in range(2):
                act.wait_ge(max_ready, 1 + m)
                nc.scalar.activation(hid[m]["exp"], psum[:, m, 2, 0:EXPERTS], ACT.Exp, bias=hid[m]["nmax"],
                                     accum_out=hid[m]["sum"]).then_inc(mlp_act, 1)

            def stage_agg(chunk):
                if chunk >= 2:
                    act.wait_ge(agg_stored[chunk % 2], 16 * (chunk // 2))
                to = outb[:, chunk % 2, :].rearrange("p (k n) -> p k n", k=4)
                act.wait_ge(agg_pe, 2 * chunk + 1)
                nc.scalar.copy(to[:, 1:3, :], psum[:, chunk % 2, 1:3, :]).then_inc(agg_act, 1)
                act.wait_ge(agg_pe, 2 * chunk + 2)
                nc.scalar.copy(to[:, 0, :], psum[:, chunk % 2, 0, :])
                nc.scalar.copy(to[:, 3, :], psum[:, chunk % 2, 3, :]).then_inc(agg_act, 1)

            def copy_lot(n, lot, last=LOTS - 1):
                if lot == 0:
                    act.wait_ge(x_loaded, 16 * PB * (n + 1))
                    if not (isinstance(n, int) and n == 0):
                        act.wait_ge(dif0_ready, 4 * n)
                size = len(COPIES) // LOTS
                for p, g in COPIES[lot * size:(lot + 1) * size]:
                    dst, src = phase_copy(p, g)
                    c = nc.scalar.copy(dst, src)
                if lot == last:
                    c.then_inc(phased, 1)

            def half_of(v, stage, j):
                act.wait_ge(kind_done, 4 * stage + 1)
                if not (isinstance(stage, int) and stage < 2):
                    act.wait_ge(mid_ready, 2 * (stage - 1))
                for b in range(PB):
                    a = nc.scalar.activation(half[:, j % 2, b * R:(b + 1) * R], psum[:, j % 2, 1, b * R:(b + 1) * R],
                                             ACT.Identity, bias=bias_now[:, v, b, CONV_BIAS[v]:CONV_BIAS[v] + 1])
                a.then_inc(half_ready, 1)

            for lot in range(PH):
                copy_lot(0, lot, PH - 1)
            for c in range(CHUNKS):
                stage_agg(c)

            def pick_biases(i):
                if is_back(i):
                    act.wait_ge(xph1_ready, PB * GROUPS * i)
                if not (isinstance(i, int) and i <= 1):
                    act.wait_ge(out_ready, PB * (i - 1))
                act.wait_ge(bias_ready, 4)
                for back in range(2):
                    if is_back(i) if back else is_front(i):
                        nc.scalar.copy(bias_now[:, back], bias_table[:, bass.ds(PB * (i - back), PB), :]
                                       ).then_inc(bias_picked, 1)
                act.wait_ge(bias_picked, 1 if isinstance(i, int) and i == 0 else
                            2 * i + (0 if isinstance(i, int) and i == PAIRS else 1))

            def step(i):
                pick_biases(i)
                if is_front(i):
                    for j in range(PH):
                        if isinstance(i, int) and i == 1:
                            stage_agg(CHUNKS + j)
                        half_of(0, stage0(i, j), j)
                        if has(i, 1):
                            copy_lot(i + 1, j)
                if is_back(i):
                    for j in range(PH):
                        if isinstance(i, int) and i == 1:
                            stage_agg(CHUNKS + PH + j)
                        half_of(1, stage2(i - 1, j), j)
                        if has(i, 1):
                            copy_lot(i + 1, PH + j)
                else:
                    for j in range(PH):
                        copy_lot(1, PH + j)
                if is_front(i):
                    if is_back(i):
                        act.wait_ge(dif2_ready, 4 * i)
                    else:
                        act.wait_ge(parts_stored[1], 16 * (PARTS + 1))
                    for b in range(PB):
                        for g in range(GROUPS):
                            act.wait_ge(mix1_done, PB * GROUPS * i + GROUPS * b + g + 1)
                            nc.scalar.activation(xph[1][:, g, b, 1:S + 1], psum[:, b, g, :], ACT.Identity,
                                                 bias=bias_now[:, 0, b, MIX1_BIAS + g:MIX1_BIAS + g + 1]
                                                 ).then_inc(xph1_ready, 1)
                if is_back(i):
                    for b in range(PB):
                        act.wait_ge(mix3_done, PB * (i - 1) + b + 1)
                        if not (isinstance(i, int) and i == 1):
                            act.wait_ge(out_stored[b], 16 * (i - 1))
                        nc.scalar.activation(outb[:, b, :].rearrange("p (s j) -> p j s", j=PH), psum[:, b, :, :],
                                             ACT.Identity, bias=bias_now[:, 1, b, MIX3_BIAS:MIX3_BIAS + 1]
                                             ).then_inc(out_ready, 1)

            pipeline(act, step)

        @block.vector
        def _(dve):
            chain = [0]

            def link(ins):
                chain[0] += 1
                ins.then_inc(dve_step, 1)
                dve.wait_ge(dve_step, chain[0])

            nc.vector.memset(ones, 1.0).then_inc(filled, 1)

            def clear_edges(v):
                edge = xph[v][:].rearrange("p g b s -> p (g b) s")
                link(nc.vector.memset(edge[:, :, 0:1], 0.0))
                link(nc.vector.memset(edge[:, :, S + 1:S + 2], 0.0))

            clear_edges(0)
            for m in range(2):
                link(nc.vector.memset(hid[m]["rows"], 1.0))

            def split(m):
                dve.wait_ge(experts_loaded[m], 16)
                for q in range(PARTS - 1):
                    link(nc.vector.tensor_copy(part[q][m], rest[m]))
                    link(nc.vector.tensor_tensor(rest[m], rest[m], part[q][m], ALU.subtract))
                nc.vector.tensor_copy(part[PARTS - 1][m], rest[m]).then_inc(parts_ready, 1)

            dve.wait_ge(par_loaded, PAR_LOADS)
            link(nc.vector.tensor_copy(eye16, eye_sb))
            split(0)
            for m in range(2):
                dve.wait_ge(mlp_pe, 5 + m)
                nc.vector.tensor_reduce(hid[m]["nmax"], psum[:, m, 2, 0:EXPERTS], AX.X, ALU.max,
                                        negate=True).then_inc(max_ready, 1)
            for m in range(2):
                h = hid[m]
                dve.wait_ge(mlp_act, 5 + m)
                link(nc.vector.reciprocal(h["inv"], h["sum"]))
                link(nc.vector.tensor_scalar(h["att"], h["exp"], h["inv"], None, ALU.mult))
                left = h["att"]
                for q in range(PARTS):
                    link(nc.vector.tensor_copy(h["part"][q], left))
                    if q < PARTS - 1:
                        link(nc.vector.tensor_tensor(h["rest"][q], left, h["part"][q], ALU.subtract))
                        left = h["rest"][q]
                for qa in range(PARTS):
                    for qe in range(PARTS):
                        at = (PARTS * qa + qe) * EXPERTS
                        last = nc.vector.tensor_copy(h["rows"][:, at:at + EXPERTS], h["part"][qa])
                last.then_inc(mlp_dve, 1)
            for m in range(2):
                dve.wait_ge(mlp_pe, 8 + 2 * m)
                nc.vector.tensor_copy(hid[m]["att_t"][0:EXPERTS, :],
                                      psum[0:EXPERTS, m, 3, 0:B]).then_inc(mlp_dve, 1)
                nc.vector.tensor_copy(hid[m]["rows_t"][:], psum[0:ROWS, m, 3, B:2 * B]).then_inc(mlp_dve, 1)
            for v in range(2):
                dve.wait_ge(bias_pe, v + 1)
                nc.vector.tensor_scalar(bias_table[:, :, CONV_BIAS[v]], psum[:, v, 0, 0:B], fside_sb, None,
                                        ALU.add).then_inc(bias_ready, 1)
            dve.wait_ge(bias_pe, 3)
            nc.vector.tensor_copy(bias_table[:, :, MIX3_BIAS], psum[:, 0, 2, 0:B]).then_inc(bias_ready, 1)
            dve.wait_ge(bias_pe, 4)
            nc.vector.tensor_copy(
                bias_table[:, :, MIX1_BIAS:MIX1_BIAS + GROUPS].rearrange("p b g -> p g b"),
                psum[:, 1, 2, :].rearrange("p (g b) -> p g b", g=GROUPS)).then_inc(bias_ready, 1)

            def sums(v, kind, ready):
                a = xph[v][:].rearrange("p g b s -> p (g b) s")
                d = [a[:, :, q:q + 2 * R - 1:2] for q in range(4)]
                in0, in1, op = {0: (d[0], d[2], ALU.subtract), 1: (d[1], d[2], ALU.add),
                                2: (d[2], d[1], ALU.subtract), 3: (d[1], d[3], ALU.subtract)}[kind]
                nc.vector.tensor_tensor(dif[v][:, kind].rearrange("p g b r -> p (g b) r"), in0, in1,
                                        op).then_inc(ready, 1)

            def outputs(v, stage, j):
                o = y[v][:, j]
                h, u, w = half[:, j % 2, :], mid[:, j % 2, 0, :], mid[:, j % 2, 1, :]
                k0, k2, k3 = (psum[:, j % 2, k, :] for k in (0, 2, 3))
                dve.wait_ge(kind_done, 4 * stage + 2)
                dve.wait_ge(half_ready, stage + 1)
                if not (isinstance(stage, int) and stage < 2):
                    dve.wait_ge(y_ready, stage - 1)
                nc.vector.tensor_tensor(u, k2, h, ALU.add).then_inc(mid_ready, 1)
                nc.vector.tensor_tensor(w, h, k2, ALU.subtract).then_inc(mid_ready, 1)
                dve.wait_ge(kind_done, 4 * stage + 3)
                dve.wait_ge(mid_ready, 2 * stage + 1)
                nc.vector.tensor_tensor(o[:, :, 0:S:2], k0.rearrange("p (b r) -> p b r", b=PB),
                                        u.rearrange("p (b r) -> p b r", b=PB), ALU.add)
                dve.wait_ge(kind_done, 4 * stage + 4)
                dve.wait_ge(mid_ready, 2 * stage + 2)
                nc.vector.tensor_tensor(o[:, :, 1:S:2], w.rearrange("p (b r) -> p b r", b=PB),
                                        k3.rearrange("p (b r) -> p b r", b=PB), ALU.subtract).then_inc(y_ready, 1)

            dve.wait_ge(x_loaded, 16 * PB)
            for p, g in COPIES[len(COPIES) // 2:]:
                dst, src = phase_copy(p, g)
                last = nc.vector.tensor_copy(dst, src)
            last.then_inc(phased, 1)
            dve.wait_ge(phased, 2)
            for kind in KIND_ORDER:
                sums(0, kind, dif0_ready)
            split(1)

            def first_sums2(n):
                dve.wait_ge(xph1_ready, PB * GROUPS * (n + 1))
                if not (isinstance(n, int) and n == 0):
                    dve.wait_ge(kind_done, 4 * stage2(n - 1, PH - 1) + 4)
                sums(1, KIND_ORDER[0], dif2_ready)

            def step(i):
                if is_front(i):
                    for j in range(PH):
                        if j == 0 and is_back(i):
                            dve.wait_ge(mix1_done, PB * GROUPS * i)
                        outputs(0, stage0(i, j), j)
                        if is_back(i) and j < PH - 1:
                            sums(1, KIND_ORDER[j + 1], dif2_ready)
                else:
                    for kind in KIND_ORDER[1:]:
                        sums(1, kind, dif2_ready)
                if is_back(i):
                    for j in range(PH):
                        if j == 0 and not (isinstance(i, int) and i == 1):
                            dve.wait_ge(mix3_done, PB * (i - 1))
                        outputs(1, stage2(i - 1, j), j)
                if has(i, 1):
                    dve.wait_ge(phased, i + 3)
                    dve.wait_ge(kind_done, 4 * stage0(i, PH - 1) + 4)
                    for kind in KIND_ORDER:
                        sums(0, kind, dif0_ready)
                if is_front(i):
                    if not is_back(i):
                        dve.wait_ge(parts_stored[1], 16 * (PARTS + 1))
                        clear_edges(1)
                    first_sums2(i)

            pipeline(dve, step)


def kernel(x, cond_128, fside_S_0, L0_cond_weight, L0_cond_c_weight, L1_cond_W0, L1_cond_b0, L1_cond_W1, L1_cond_b1,
           L1_cond_W2, L1_cond_b2, L1_cond_weight, L1_cond_bias_k, L2_cond_weight, L2_cond_c_weight, L3_cond_W0,
           L3_cond_b0, L3_cond_W1, L3_cond_b1, L3_cond_W2, L3_cond_b2, L3_cond_weight, L3_cond_bias_k):
    import numpy as np
    import concourse.bacc as bacc
    from concourse.bass_utils import run_bass_kernel_spmd

    nc = bacc.Bacc("TRN2", target_bir_lowering=False, num_devices=1)
    arrays = {}

    def give(name, a):
        a = np.ascontiguousarray(a)
        arrays[name] = a
        return nc.dram_tensor(name, a.shape, mybir.dt.from_np(a.dtype), kind="ExternalInput").ap()

    def taps(w):
        w = np.asarray(w)
        o, c, k = w.shape
        return w.reshape(o // c, c, c, k).transpose(3, 2, 0, 1)

    def expert_rows(w):
        w = np.asarray(w)
        return w[..., 0].transpose(0, 2, 1).reshape(w.shape[0], -1)

    def col(a):
        return np.asarray(a).reshape(-1, 1)

    x = np.asarray(x)
    p = x.shape[1]
    eye = np.eye(p, dtype=np.float32)
    wide = [np.asarray(cond_128).T, eye, eye.reshape(p, 4, -1)[:, ::-1].reshape(p, p), col(fside_S_0),
            np.asarray(L0_cond_c_weight).T, np.asarray(L2_cond_c_weight).T,
            L1_cond_W0, L1_cond_W1, L1_cond_W2, col(L1_cond_b0), col(L1_cond_b1),
            L3_cond_W0, L3_cond_W1, L3_cond_W2, col(L3_cond_b0), col(L3_cond_b1)]
    args = {
        "x": give("x", x),
        "wide": give("wide", np.concatenate([np.asarray(a) for a in wide], axis=1)),
        "bias_k": give("bias_k", np.stack([np.asarray(L1_cond_bias_k), np.asarray(L3_cond_bias_k)], axis=1)),
        "b2": give("b2", np.stack([np.asarray(L1_cond_b2), np.asarray(L3_cond_b2)])[None]),
        "experts": [give("experts_1", expert_rows(L1_cond_weight)), give("experts_3", expert_rows(L3_cond_weight))],
        "conv_w": [give("conv_w0", taps(L0_cond_weight)), give("conv_w2", taps(L2_cond_weight))],
        "out": nc.dram_tensor("out", x.shape, F32, kind="ExternalOutput").ap(),
    }
    conditioned_layers(nc, **args)
    r = run_bass_kernel_spmd(nc, [arrays], core_ids=[0])
    return r.results[0]["out"]
```

```python
from contextlib import ExitStack

import concourse.bass as bass
from concourse import mybir

F32 = mybir.dt.float32
F32R = mybir.dt.float32r
BF16 = mybir.dt.bfloat16
ALU = mybir.AluOpType
ACT = mybir.ActivationFunctionType
AX = mybir.AxisListType

P = 128
GROUPS = 4
CG = P // GROUPS
PH = 4
HALVES = 2
BANK = 512
PB = 2
CONV_BIAS, MIX1_BIAS, MIX3_BIAS, BIASES = (0, 1), 2, 6, 7
KIND_ORDER = (1, 2, 0, 3)


def conditioned_layers(nc, x, wide, bias_k, b2, experts, conv_w, out):
    B, C, L = x.shape
    S = L // PH
    R = S // 2
    TAPS = conv_w[0].shape[0]
    HALO = TAPS // 2
    PAIRS = B // PB
    EXPERTS = bias_k.shape[0]
    PARTS = 3
    ROWS = PARTS * PARTS * EXPERTS + 1
    SPLIT = EXPERTS * P * P // P
    CHUNK = 2 * BANK
    CHUNKS = P * P // CHUNK
    assert C == P and B == P and S == BANK and PB * R == BANK and TAPS == 2 * PH + 1 and PAIRS > 4

    mix_dram = [nc.dram_tensor(f"mix_dram{m}", (B, P * P), F32).ap() for m in range(2)]

    parts_dram = [nc.dram_tensor(f"parts_dram{m}", (PARTS * EXPERTS + 1, P * P), BF16).ap() for m in range(2)]

    with ExitStack() as ctx:
        def sb(name, shape, dtype=F32):
            return ctx.enter_context(nc.sbuf_tensor(name, shape, dtype))

        def sem(name):
            return ctx.enter_context(nc.semaphore(name))

        xin = sb("xin", [P, PB, L])
        xph = [sb(f"xph{v}", [P, GROUPS, PB, S + 2]) for v in range(2)]
        dif = [sb(f"dif{v}", [P, 4, GROUPS, PB, R]) for v in range(2)]
        y0 = sb("y0", [P, PH, PB, S])
        y2 = sb("y2", [P, 2, PB, S])
        y2_high = sb("y2_high", [P, PH, PB, S], F32R)
        y2_low = sb("y2_low", [P, PH, PB, S], F32R)
        outb = y0[:].rearrange("p j b s -> p (j b s)").rearrange("p (b l) -> p b l", b=PB)
        half = sb("half", [P, 2, BANK])
        mid = sb("mid", [P, 2, BANK])
        rows = sb("rows", [ROWS, 2, CHUNK], BF16)
        wino = [sb(f"wino{v}", [P, 4, PH, GROUPS, CG]) for v in range(2)]
        mixw = [sb(f"mixw{m}", [P, PB, P]) for m in range(2)]
        mixw3_high = sb("mixw3_high", [P, PB, P], F32R)
        mixw3_low = sb("mixw3_low", [P, PB, P], F32R)
        bias_table = sb("bias_table", [P, B, BIASES])
        bias_now = sb("bias_now", [P, 2, PB, BIASES])
        psum = ctx.enter_context(nc.psum_tensor("psum", [P, HALVES, 4, BANK], F32))

        host = [y0[:].rearrange("p j b s -> p (j b s)"), dif[1][:].rearrange("p k g b r -> p (k g b r)")]
        blocks = [host[v][:, 0:3 * BANK].rearrange("p (m j g o) -> p m j g o", m=3, g=GROUPS, j=PH)
                  for v in range(2)]
        flat = xph[1][:].rearrange("p g b s -> p (g b s)")
        part = [[flat[:, (2 * q + m) * SPLIT // 2:(2 * q + m + 1) * SPLIT // 2].bitcast(BF16) for m in range(2)]
                for q in range(PARTS)]
        staging = [y2[:, a].rearrange("p b s -> p (b s)") for a in range(2)]
        staging += [host[1][:, 3 * GROUPS * BANK + a * CHUNK:3 * GROUPS * BANK + (a + 1) * CHUNK] for a in range(2)]
        STAGINGS = len(staging)
        assert PB * S == CHUNK and GROUPS * BANK == 2 * CHUNK
        used = [3 * BANK, 3 * BANK]

        def carve(v, cols):
            used[v] += cols
            return host[v][:, used[v] - cols:used[v]]

        ones = carve(0, P)
        rest = [carve(1, SPLIT) for _ in range(2)]
        wide_sb = carve(1, wide.shape[1])
        wide_at = [0]

        def field(cols):
            wide_at[0] += cols
            return wide_sb[:, wide_at[0] - cols:wide_at[0]]

        emb_sb, eye_sb, eye_down, fside_sb = field(B), field(P), field(P), field(1)
        ctx_sb = [field(P) for _ in range(2)]
        par = [{"w0": field(P), "w1": field(P), "w2": field(EXPERTS), "b0": field(1), "b1": field(1)}
               for _ in range(2)]
        assert wide_at[0] == wide.shape[1]
        bias_k_sb = carve(0, 2 * P)[0:EXPERTS, :].rearrange("k (m o) -> k m o", m=2)
        b2_sb = carve(0, 2 * EXPERTS)[0:1, :].rearrange("a (m k) -> a m k", m=2)
        eye16 = carve(1, P // 2).bitcast(BF16)
        assert used[1] <= 3 * GROUPS * BANK
        hid = [{"h": carve(0, P), "h1": carve(0, P), "nmax": carve(0, 1), "exp": carve(0, EXPERTS),
                "sum": carve(0, 1), "inv": carve(0, 1), "att": carve(0, EXPERTS), "att_t": carve(0, P),
                "part": [carve(0, EXPERTS // 2).bitcast(BF16) for _ in range(PARTS)],
                "rest": [carve(0, EXPERTS) for _ in range(PARTS - 1)], "rows": carve(0, ROWS),
                "rows_t": sb(f"att_rows_t{m}", [ROWS, P], BF16)} for m in range(2)]

        par_loaded = sem("par_loaded")
        taps_loaded = [sem(f"taps_loaded{v}") for v in range(2)]
        taps_cleared = sem("taps_cleared")
        experts_loaded = [sem(f"experts_loaded{m}") for m in range(2)]
        parts_ready = sem("parts_ready")
        parts_stored = [sem(f"parts_stored{m}") for m in range(2)]
        rows_loaded = [sem(f"rows_loaded{v}") for v in range(2)]
        wino_step = [sem(f"wino_step{v}") for v in range(2)]
        wino_ready = [sem(f"wino_ready{v}") for v in range(2)]
        dve_step = sem("dve_step")
        filled = sem("filled")
        mlp_pe = sem("mlp_pe")
        mlp_act = sem("mlp_act")
        max_ready = sem("max_ready")
        mlp_dve = sem("mlp_dve")
        bias_pe = sem("bias_pe")
        bias_ready = sem("bias_ready")
        agg_pe = sem("agg_pe")
        agg_act = sem("agg_act")
        agg_stored = [sem(f"agg_stored{v}") for v in range(STAGINGS)]

        bias_picked = sem("bias_picked")
        x_loaded = sem("x_loaded")
        phased = sem("phased")
        dif0_ready = sem("dif0_ready")
        dif2_ready = sem("dif2_ready")
        kind_done = sem("kind_done")
        half_ready = sem("half_ready")
        mid_ready = sem("mid_ready")
        y_ready = sem("y_ready")
        mix1_loaded = sem("mix1_loaded")
        mix3_loaded = sem("mix3_loaded")
        y2_high_ready = sem("y2_high_ready")
        y2_low_ready = sem("y2_low_ready")
        mixw3_high_ready = sem("mixw3_high_ready")
        mixw3_low_ready = sem("mixw3_low_ready")
        mix1_done = sem("mix1_done")
        xph1_ready = sem("xph1_ready")
        mix3_done = sem("mix3_done")
        out_ready = sem("out_ready")
        out_stored = [sem(f"out_stored{b}") for b in range(PB)]

        def stage0(i, j):
            return j if isinstance(i, int) and i == 0 else 8 * i - 4 + j

        def stage2(n, j):
            return 8 * n + 8 + j - (4 if isinstance(n, int) and n == PAIRS - 1 else 0)

        def pipeline(eng, step):
            step(0)
            step(1)
            with eng.Fori(2, PAIRS - 2) as i:
                step(i)
            step(PAIRS - 2)
            step(PAIRS - 1)
            step(PAIRS)

        def is_front(i):
            return not (isinstance(i, int) and i >= PAIRS)

        def is_back(i):
            return not (isinstance(i, int) and i < 1)

        def has(i, ahead):
            return not (isinstance(i, int) and i + ahead >= PAIRS)

        COPIES = [(p, g) for p in range(PH) for g in range(GROUPS)]
        LOTS = 2 * PH

        def phase_copy(p, g):
            dst = xph[0][CG * p:CG * (p + 1), g, :, 1:S + 1]
            src = xin[CG * g:CG * (g + 1), :, p:p + PH * (S - 1) + 1:PH]
            return dst, src

        PAR_LOADS = 16 * 3
        ALONE = CHUNKS - 2 * PH
        assert ALONE % 2 == 0 and CHUNKS % STAGINGS == 0

        def chunks_of(i):
            return ALONE + CHUNKS * i

        block = ctx.enter_context(nc.Block())

        @block.sync
        def _(sp):
            for v in range(2):
                sp.wait_ge(taps_cleared, v + 1)
                line = blocks[v].rearrange("p m j g o -> p (m j) g o")
                for p in range(PH):
                    sp.dma_start(line[CG * p:CG * (p + 1), PH - 1 - p:PH - 1 - p + TAPS],
                                 conv_w[v].rearrange("k c g o -> c k g o")).then_inc(taps_loaded[v], 16)
                if v == 0:
                    for b in range(PB):
                        sp.dma_start(xin[:, b, :], x[b]).then_inc(x_loaded, 16)

            def load_x(n):
                sp.wait_ge(phased, n + 1)
                for b in range(PB):
                    sp.dma_start(xin[:, b, :], x[PB * n + b]).then_inc(x_loaded, 16)

            def store_parts(m):
                sp.wait_ge(parts_ready, m + 1)
                for q in range(PARTS):
                    sp.dma_start(parts_dram[m][q * EXPERTS:(q + 1) * EXPERTS, :].rearrange(
                        "k (q c) -> (k q) c", c=SPLIT), part[q][m]).then_inc(parts_stored[m], 16)
                sp.dma_start(parts_dram[m][PARTS * EXPERTS, :].rearrange("(i o) -> i o", i=P),
                             eye16).then_inc(parts_stored[m], 16)
                sp.wait_ge(parts_stored[m], 16 * (PARTS + 1))
                for c in range(2):
                    load_rows(m, c)

            def load_rows(m, c):
                chunk = m * CHUNKS + c
                if chunk >= 2:
                    sp.wait_ge(agg_pe, chunk - 1)
                for qa in range(PARTS):
                    n = PARTS * EXPERTS + (1 if qa == PARTS - 1 else 0)
                    sp.dma_start(rows[PARTS * EXPERTS * qa:PARTS * EXPERTS * qa + n, c % 2, :],
                                 parts_dram[m][0:n, c * CHUNK:(c + 1) * CHUNK]).then_inc(rows_loaded[c % 2], 16)

            def store_agg(m):
                for c in range(CHUNKS):
                    chunk = m * CHUNKS + c
                    if c + 2 < CHUNKS:
                        load_rows(m, c + 2)
                    sp.wait_ge(agg_act, 2 * (chunk + 1))
                    sp.dma_start(mix_dram[m][:, c * CHUNK:(c + 1) * CHUNK], staging[c % STAGINGS]
                                 ).then_inc(agg_stored[c % STAGINGS], 16)
                for v in range(STAGINGS):
                    sp.wait_ge(agg_stored[v], 16 * CHUNKS * (m + 1) // STAGINGS)

            def load_mix(m, n):
                if not (isinstance(n, int) and n == 0):
                    if m == 0:
                        sp.wait_ge(mix1_done, PB * GROUPS * n)
                    else:
                        sp.wait_ge(mixw3_low_ready, n)
                for b in range(PB):
                    src = mix_dram[m].rearrange("b (i o) -> b i o", i=P)
                    sp.dma_start(mixw[m][:, b, :], src[PB * n + b]).then_inc((mix1_loaded, mix3_loaded)[m], 16)

            store_parts(0)
            load_x(1)
            store_agg(0)
            load_mix(0, 0)
            store_parts(1)

            def step(i):
                if isinstance(i, int) and i == 1:
                    store_agg(1)
                    load_mix(1, 0)
                if has(i, 2):
                    load_x(i + 2)
                if has(i, 1):
                    load_mix(0, i + 1)
                if is_back(i):
                    for b in range(PB):
                        sp.wait_ge(out_ready, PB * (i - 1) + b + 1)
                        sp.dma_start(out[PB * (i - 1) + b], outb[:, b, :]).then_inc(out_stored[b], 16)
                    if has(i, 0):
                        load_mix(1, i)

            pipeline(sp, step)
            for b in range(PB):
                sp.wait_ge(out_stored[b], 16 * PAIRS)

        def weights_of(v, eng, done):
            count = 0

            def link(ins):
                nonlocal count
                count += 1
                ins.then_inc(done, 1)
                eng.wait_ge(done, count)

            eng.wait_ge(par_loaded, PAR_LOADS)
            eng.wait_ge(taps_loaded[v], 16 * PH)
            before, here, after = (blocks[v][:, m].rearrange("p j g o -> p (j g o)") for m in range(3))
            w = [wino[v][:, k].rearrange("p j g o -> p (j g o)") for k in range(4)]
            for g in range(GROUPS):
                link(eng.tensor_tensor(blocks[v][:, 1, :, g, :], blocks[v][:, 1, :, g, :],
                                       eye_down.rearrange("p (j o) -> p j o", j=PH), ALU.add))
            link(eng.tensor_copy(w[0], before))
            link(eng.tensor_copy(w[3], after))
            link(eng.tensor_tensor(before, before, after, ALU.add))
            link(eng.tensor_tensor(w[1], before, here, ALU.add))
            link(eng.tensor_tensor(w[2], before, here, ALU.subtract))
            link(eng.tensor_scalar(w[1], w[1], 0.5, None, ALU.mult))
            eng.tensor_scalar(w[2], w[2], 0.5, None, ALU.mult).then_inc(wino_ready[v], 1)

        @block.gpsimd
        def _(pool):
            for v in range(2):
                pool.memset(blocks[v].rearrange("p m j g o -> p (m j g o)"), 0.0).then_inc(taps_cleared, 1)
            for v in range(2):
                weights_of(v, pool, wino_step[v])

            def step(i):
                if is_back(i):
                    pool.wait_ge(mixw3_high_ready, i)
                    pool.tensor_tensor(mixw3_low[:], mixw[1][:], mixw3_high[:].bitcast(F32),
                                       ALU.subtract).then_inc(mixw3_low_ready, 1)
                    for j in range(PH):
                        pool.wait_ge(y2_high_ready, PH * (i - 1) + j + 1)
                        pool.tensor_tensor(y2_low[:, j], y2[:, j % 2], y2_high[:, j].bitcast(F32),
                                           ALU.subtract).then_inc(y2_low_ready, 1)

            pipeline(pool, step)

        @block.tensor
        def _(pe):
            pe.wait_ge(par_loaded, PAR_LOADS)
            pe.wait_ge(filled, 1)
            for m in range(2):
                pe.matmul(psum[:, m, 0, 0:B], par[m]["w0"], emb_sb, start=True, stop=True).then_inc(mlp_pe, 1)
            for m in range(2):
                pe.wait_ge(mlp_act, 1 + m)
                pe.matmul(psum[:, m, 1, 0:B], par[m]["w1"], hid[m]["h"], start=True, stop=True).then_inc(mlp_pe, 1)
            for m in range(2):
                pe.wait_ge(mlp_act, 3 + m)
                pe.matmul(psum[:, m, 2, 0:EXPERTS], hid[m]["h1"], par[m]["w2"], start=True, stop=False)
                pe.matmul(psum[:, m, 2, 0:EXPERTS], ones[0:1, 0:B], b2_sb[:, m, :], start=False,
                          stop=True).then_inc(mlp_pe, 1)
            for m in range(2):
                pe.wait_ge(mlp_dve, 1 + m)
                pe.transpose(psum[0:EXPERTS, m, 3, 0:B], hid[m]["att"], eye_sb).then_inc(mlp_pe, 1)
                pe.transpose(psum[0:ROWS, m, 3, B:2 * B], hid[m]["rows"], eye_sb).then_inc(mlp_pe, 1)
            for v in range(2):
                pe.matmul(psum[:, v, 0, 0:B], ctx_sb[v], emb_sb, start=True, stop=True).then_inc(bias_pe, 1)
            pe.wait_ge(mlp_dve, 6)
            pe.matmul(psum[:, 0, 2, 0:B], bias_k_sb[:, 1, :], hid[1]["att_t"][0:EXPERTS, :],
                      start=True, stop=True).then_inc(bias_pe, 1)
            for j in range(PH):
                for g in range(GROUPS):
                    mm = pe.matmul(psum[CG * j:CG * (j + 1), 1, 2, B * g:B * (g + 1)],
                                   bias_k_sb[:, 0, CG * g:CG * (g + 1)],
                                   hid[0]["att_t"][0:EXPERTS, :], start=True, stop=True)
            mm.then_inc(bias_pe, 1)
            pe.wait_ge(bias_ready, 4)

            def aggregate(chunk, h):
                m, c = divmod(chunk, CHUNKS)
                pe.wait_ge(rows_loaded[c % 2], 16 * PARTS * (chunk // 2 + 1))
                for n, k in enumerate((0, 3)):
                    mm = pe.matmul(psum[:, h, k, :], hid[m]["rows_t"][:], rows[:, c % 2, n * BANK:(n + 1) * BANK],
                                   start=True, stop=True)
                mm.then_inc(agg_pe, 1)

            for c in range(ALONE):
                if c >= 2:
                    pe.wait_ge(agg_act, 2 * (c - 1))
                aggregate(c, c % 2)
            pe.wait_ge(wino_ready[0], 1)

            def conv(v, j, free):
                for pos, kind in enumerate(KIND_ORDER):
                    free(pos)
                    for g in range(GROUPS):
                        mm = pe.matmul(psum[CG * g:CG * (g + 1), j % 2, kind, :], wino[v][:, kind, PH - 1 - j, g, :],
                                       dif[v][:, kind, g, :, :].rearrange("p b r -> p (b r)"),
                                       start=True, stop=True)
                    mm.then_inc(kind_done, 1)

            def mix1(b):
                for g in range(GROUPS):
                    for j in range(PH):
                        mm = pe.matmul(psum[CG * j:CG * (j + 1), b, g, :], mixw[0][:, b, CG * g:CG * (g + 1)],
                                       y0[:, j, b, :], start=True, stop=True)
                    mm.then_inc(mix1_done, 1)

            def mix3(b):
                for j in range(PH):
                    pe.matmul(psum[:, b, j, :], mixw3_high[:, b, :], y2_high[:, j, b, :], start=True, stop=False)
                    pe.matmul(psum[:, b, j, :], mixw3_high[:, b, :], y2_low[:, j, b, :], start=False, stop=False)
                    mm = pe.matmul(psum[:, b, j, :], mixw3_low[:, b, :], y2_high[:, j, b, :], start=False, stop=True)
                mm.then_inc(mix3_done, 1)

            def step(i):
                first = isinstance(i, int) and i == 0
                second = isinstance(i, int) and i == 1

                def stage_with_chunks(v, stage, j, free):
                    chunk = chunks_of(i) + 2 * j
                    if j < 2:
                        pe.wait_ge(agg_act, 2 * chunks_of(i))
                    else:
                        pe.wait_ge(y_ready, stage - 1)
                    aggregate(chunk, j % 2)

                    def with_second(pos):
                        free(pos)
                        if pos == 2:
                            pe.wait_ge(agg_act, 2 * (chunk + 1))
                            aggregate(chunk + 1, j % 2)
                        if pos >= 2:
                            pe.wait_ge(agg_act, 2 * (chunk + 1) + pos - 1)

                    conv(v, j, with_second)

                def conv_free(stage):
                    def free(pos):
                        if pos == 0:
                            pe.wait_ge(half_ready, stage - 1)
                        if pos == 1:
                            pe.wait_ge(mid_ready, 2 * (stage - 1))
                        if pos == 2:
                            pe.wait_ge(y_ready, stage - 1)
                    return free

                if is_front(i):
                    for j in range(PH):
                        def free(pos, j=j):
                            if j == 0:
                                pe.wait_ge(dif0_ready, 4 * i + pos + 1)
                            if j < 2 and pos == 0 and not first:
                                if not second:
                                    pe.wait_ge(out_ready, PB * (i - 2) + j + 1)
                            if j >= 2:
                                conv_free(stage0(i, j))(pos)
                        if first or second:
                            stage_with_chunks(0, stage0(i, j), j, free)
                        else:
                            conv(0, j, free)
                if is_back(i):
                    for j in range(PH):
                        def free(pos, j=j):
                            if j == 0:
                                pe.wait_ge(dif2_ready, 4 * (i - 1) + pos + 1)
                            if j >= 2:
                                conv_free(stage2(i - 1, j))(pos)
                            elif is_front(i):
                                conv_free(stage2(i - 1, j))(pos)
                            elif pos == 0:
                                pe.wait_ge(out_ready, PB * (i - 2) + j + 1)
                        conv(1, j, free)
                if is_front(i):
                    pe.wait_ge(y_ready, stage0(i, PH - 1) + 1)
                    pe.wait_ge(mix1_loaded, 16 * PB * (i + 1))
                    for b in range(PB):
                        if is_back(i):
                            pe.wait_ge(y_ready, stage2(i - 1, 2 + b) + 1)
                        mix1(b)
                    if not is_back(i):
                        for c in range(CHUNKS, CHUNKS + ALONE):
                            if c < CHUNKS + 2:
                                pe.wait_ge(xph1_ready, GROUPS * (c - CHUNKS + 1))
                            else:
                                pe.wait_ge(agg_act, 2 * (c - 1))
                            aggregate(c, c % 2)
                        pe.wait_ge(wino_ready[1], 1)
                if is_back(i):
                    pe.wait_ge(mixw3_low_ready, i)
                    pe.wait_ge(y2_low_ready, PH * i)
                    if not is_front(i):
                        pe.wait_ge(y_ready, stage2(i - 1, PH - 1) + 1)
                    for b in range(PB):
                        if is_front(i):
                            pe.wait_ge(xph1_ready, PB * GROUPS * i + GROUPS * (b + 1))
                        mix3(b)

            pipeline(pe, step)

        @block.scalar
        def _(act):
            act.dma_start(rest[0], experts[0].rearrange("k (q c) -> (k q) c", c=SPLIT)).then_inc(experts_loaded[0], 16)
            act.dma_start(wide_sb, wide).then_inc(par_loaded, 16)
            act.dma_start(bias_k_sb, bias_k).then_inc(par_loaded, 16)
            act.dma_start(b2_sb, b2).then_inc(par_loaded, 16)
            act.dma_start(rest[1], experts[1].rearrange("k (q c) -> (k q) c", c=SPLIT)).then_inc(experts_loaded[1], 16)
            act.wait_ge(par_loaded, PAR_LOADS)
            for layer, (bias, hout) in enumerate((("b0", "h"), ("b1", "h1"))):
                for m in range(2):
                    act.wait_ge(mlp_pe, 2 * layer + m + 1)
                    nc.scalar.activation(hid[m][hout], psum[:, m, layer, 0:B], ACT.Gelu,
                                         bias=par[m][bias]).then_inc(mlp_act, 1)
            for m in range(2):
                act.wait_ge(max_ready, 1 + m)
                nc.scalar.activation(hid[m]["exp"], psum[:, m, 2, 0:EXPERTS], ACT.Exp, bias=hid[m]["nmax"],
                                     accum_out=hid[m]["sum"]).then_inc(mlp_act, 1)

            def stage_agg(chunk, h):
                act.wait_ge(agg_pe, chunk + 1)
                to = chunk % STAGINGS
                if chunk >= STAGINGS:
                    act.wait_ge(agg_stored[to], 16 * (chunk // STAGINGS))
                nc.scalar.copy(staging[to][:, 0:BANK], psum[:, h, 0, :]).then_inc(agg_act, 1)
                nc.scalar.copy(staging[to][:, BANK:CHUNK], psum[:, h, 3, :]).then_inc(agg_act, 1)

            def copy_lot(n, lot, last=LOTS - 1):
                if lot == 0:
                    act.wait_ge(x_loaded, 16 * PB * (n + 1))
                    if not (isinstance(n, int) and n == 0):
                        act.wait_ge(dif0_ready, 4 * n)
                size = len(COPIES) // LOTS
                for p, g in COPIES[lot * size:(lot + 1) * size]:
                    dst, src = phase_copy(p, g)
                    c = nc.scalar.copy(dst, src)
                if lot == last:
                    c.then_inc(phased, 1)

            def half_of(v, stage, j):
                act.wait_ge(kind_done, 4 * stage + 1)
                if not (isinstance(stage, int) and stage < 2):
                    act.wait_ge(mid_ready, 2 * (stage - 1))
                for b in range(PB):
                    a = nc.scalar.activation(half[:, j % 2, b * R:(b + 1) * R], psum[:, j % 2, 1, b * R:(b + 1) * R],
                                             ACT.Identity, bias=bias_now[:, v, b, CONV_BIAS[v]:CONV_BIAS[v] + 1])
                a.then_inc(half_ready, 1)

            def high_matrices(n):
                act.wait_ge(mix3_loaded, 16 * PB * (n + 1))
                if not (isinstance(n, int) and n == 0):
                    act.wait_ge(mix3_done, PB * n)
                nc.scalar.copy(mixw3_high[:], mixw[1][:]).then_inc(mixw3_high_ready, 1)

            def high_of(n, j):
                act.wait_ge(y_ready, stage2(n, j) + 1)
                nc.scalar.copy(y2_high[:, j], y2[:, j % 2]).then_inc(y2_high_ready, 1)

            for lot in range(PH):
                copy_lot(0, lot, PH - 1)
            for c in range(ALONE):
                stage_agg(c, c % 2)

            def pick_biases(i):
                if is_back(i):
                    act.wait_ge(xph1_ready, PB * GROUPS * i)
                if not (isinstance(i, int) and i <= 1):
                    act.wait_ge(out_ready, PB * (i - 1))
                act.wait_ge(bias_ready, 4)
                for back in range(2):
                    if is_back(i) if back else is_front(i):
                        nc.scalar.copy(bias_now[:, back], bias_table[:, bass.ds(PB * (i - back), PB), :]
                                       ).then_inc(bias_picked, 1)
                act.wait_ge(bias_picked, 1 if isinstance(i, int) and i == 0 else
                            2 * i + (0 if isinstance(i, int) and i == PAIRS else 1))

            def step(i):
                pick_biases(i)
                if is_front(i):
                    for j in range(PH):
                        if isinstance(i, int) and i <= 1:
                            stage_agg(chunks_of(i) + 2 * j, j % 2)
                        half_of(0, stage0(i, j), j)
                        if isinstance(i, int) and i <= 1:
                            stage_agg(chunks_of(i) + 2 * j + 1, j % 2)
                        if has(i, 1):
                            copy_lot(i + 1, j)
                if is_back(i):
                    for j in range(PH):
                        half_of(1, stage2(i - 1, j), j)
                        if j == 0:
                            high_matrices(i - 1)
                        else:
                            high_of(i - 1, j - 1)
                        if has(i, 1):
                            copy_lot(i + 1, PH + j)
                    high_of(i - 1, PH - 1)
                else:
                    for j in range(PH):
                        copy_lot(1, PH + j)
                if is_front(i):
                    if is_back(i):
                        act.wait_ge(dif2_ready, 4 * i)
                    else:
                        act.wait_ge(parts_stored[1], 16 * (PARTS + 1))
                    for b in range(PB):
                        for g in range(GROUPS):
                            act.wait_ge(mix1_done, PB * GROUPS * i + GROUPS * b + g + 1)
                            nc.scalar.activation(xph[1][:, g, b, 1:S + 1], psum[:, b, g, :], ACT.Identity,
                                                 bias=bias_now[:, 0, b, MIX1_BIAS + g:MIX1_BIAS + g + 1]
                                                 ).then_inc(xph1_ready, 1)
                    if not is_back(i):
                        for c in range(CHUNKS, CHUNKS + ALONE):
                            stage_agg(c, c % 2)
                if is_back(i):
                    for b in range(PB):
                        act.wait_ge(mix3_done, PB * (i - 1) + b + 1)
                        if not (isinstance(i, int) and i == 1):
                            act.wait_ge(out_stored[b], 16 * (i - 1))
                        nc.scalar.activation(outb[:, b, :].rearrange("p (s j) -> p j s", j=PH), psum[:, b, :, :],
                                             ACT.Identity, bias=bias_now[:, 1, b, MIX3_BIAS:MIX3_BIAS + 1]
                                             ).then_inc(out_ready, 1)

            pipeline(act, step)

        @block.vector
        def _(dve):
            chain = [0]

            def link(ins):
                chain[0] += 1
                ins.then_inc(dve_step, 1)
                dve.wait_ge(dve_step, chain[0])

            nc.vector.memset(ones, 1.0).then_inc(filled, 1)

            def clear_edges(v):
                edge = xph[v][:].rearrange("p g b s -> p (g b) s")
                link(nc.vector.memset(edge[:, :, 0:1], 0.0))
                link(nc.vector.memset(edge[:, :, S + 1:S + 2], 0.0))

            clear_edges(0)
            for m in range(2):
                link(nc.vector.memset(hid[m]["rows"], 1.0))

            def split(m):
                dve.wait_ge(experts_loaded[m], 16)
                for q in range(PARTS - 1):
                    link(nc.vector.tensor_copy(part[q][m], rest[m]))
                    link(nc.vector.tensor_tensor(rest[m], rest[m], part[q][m], ALU.subtract))
                nc.vector.tensor_copy(part[PARTS - 1][m], rest[m]).then_inc(parts_ready, 1)

            dve.wait_ge(par_loaded, PAR_LOADS)
            link(nc.vector.tensor_copy(eye16, eye_sb))
            split(0)
            for m in range(2):
                dve.wait_ge(mlp_pe, 5 + m)
                nc.vector.tensor_reduce(hid[m]["nmax"], psum[:, m, 2, 0:EXPERTS], AX.X, ALU.max,
                                        negate=True).then_inc(max_ready, 1)
            for m in range(2):
                h = hid[m]
                dve.wait_ge(mlp_act, 5 + m)
                link(nc.vector.reciprocal(h["inv"], h["sum"]))
                link(nc.vector.tensor_scalar(h["att"], h["exp"], h["inv"], None, ALU.mult))
                left = h["att"]
                for q in range(PARTS):
                    link(nc.vector.tensor_copy(h["part"][q], left))
                    if q < PARTS - 1:
                        link(nc.vector.tensor_tensor(h["rest"][q], left, h["part"][q], ALU.subtract))
                        left = h["rest"][q]
                for qa in range(PARTS):
                    for qe in range(PARTS):
                        at = (PARTS * qa + qe) * EXPERTS
                        last = nc.vector.tensor_copy(h["rows"][:, at:at + EXPERTS], h["part"][qa])
                last.then_inc(mlp_dve, 1)
            dve.wait_ge(x_loaded, 16 * PB)
            for p, g in COPIES[len(COPIES) // 2:]:
                dst, src = phase_copy(p, g)
                last = nc.vector.tensor_copy(dst, src)
            last.then_inc(phased, 1)
            for m in range(2):
                dve.wait_ge(mlp_pe, 8 + 2 * m)
                nc.vector.tensor_copy(hid[m]["att_t"][0:EXPERTS, :],
                                      psum[0:EXPERTS, m, 3, 0:B]).then_inc(mlp_dve, 1)
                nc.vector.tensor_copy(hid[m]["rows_t"][:], psum[0:ROWS, m, 3, B:2 * B]).then_inc(mlp_dve, 1)
            for v in range(2):
                dve.wait_ge(bias_pe, v + 1)
                nc.vector.tensor_scalar(bias_table[:, :, CONV_BIAS[v]], psum[:, v, 0, 0:B], fside_sb, None,
                                        ALU.add).then_inc(bias_ready, 1)
            dve.wait_ge(bias_pe, 3)
            nc.vector.tensor_copy(bias_table[:, :, MIX3_BIAS], psum[:, 0, 2, 0:B]).then_inc(bias_ready, 1)
            dve.wait_ge(bias_pe, 4)
            nc.vector.tensor_copy(
                bias_table[:, :, MIX1_BIAS:MIX1_BIAS + GROUPS].rearrange("p b g -> p g b"),
                psum[:, 1, 2, :].rearrange("p (g b) -> p g b", g=GROUPS)).then_inc(bias_ready, 1)

            def sums(v, kind, ready):
                a = xph[v][:].rearrange("p g b s -> p (g b) s")
                d = [a[:, :, q:q + 2 * R - 1:2] for q in range(4)]
                in0, in1, op = {0: (d[0], d[2], ALU.subtract), 1: (d[1], d[2], ALU.add),
                                2: (d[2], d[1], ALU.subtract), 3: (d[1], d[3], ALU.subtract)}[kind]
                nc.vector.tensor_tensor(dif[v][:, kind].rearrange("p g b r -> p (g b) r"), in0, in1,
                                        op).then_inc(ready, 1)

            def outputs(v, stage, j):
                o = y2[:, j % 2] if v else y0[:, j]
                h, u, w = half[:, j % 2, :], mid[:, 0, :], mid[:, 1, :]
                k0, k2, k3 = (psum[:, j % 2, k, :] for k in (0, 2, 3))
                dve.wait_ge(kind_done, 4 * stage + 2)
                dve.wait_ge(half_ready, stage + 1)
                if not (isinstance(stage, int) and stage < 1):
                    dve.wait_ge(y_ready, stage)
                nc.vector.tensor_tensor(u, k2, h, ALU.add).then_inc(mid_ready, 1)
                nc.vector.tensor_tensor(w, h, k2, ALU.subtract).then_inc(mid_ready, 1)
                dve.wait_ge(kind_done, 4 * stage + 3)
                dve.wait_ge(mid_ready, 2 * stage + 1)
                nc.vector.tensor_tensor(o[:, :, 0:S:2], k0.rearrange("p (b r) -> p b r", b=PB),
                                        u.rearrange("p (b r) -> p b r", b=PB), ALU.add)
                dve.wait_ge(kind_done, 4 * stage + 4)
                dve.wait_ge(mid_ready, 2 * stage + 2)
                nc.vector.tensor_tensor(o[:, :, 1:S:2], w.rearrange("p (b r) -> p b r", b=PB),
                                        k3.rearrange("p (b r) -> p b r", b=PB), ALU.subtract).then_inc(y_ready, 1)

            dve.wait_ge(phased, 2)
            for kind in KIND_ORDER:
                sums(0, kind, dif0_ready)
            split(1)

            def first_sums2(n):
                dve.wait_ge(xph1_ready, PB * GROUPS * (n + 1))
                if not (isinstance(n, int) and n == 0):
                    dve.wait_ge(kind_done, 4 * stage2(n - 1, PH - 1) + 4)
                sums(1, KIND_ORDER[0], dif2_ready)

            def step(i):
                if is_front(i):
                    for j in range(PH):
                        last_kind = isinstance(i, int) and i == 1 and j == PH - 2
                        if is_back(i) and j < PH - 1 and not last_kind:
                            sums(1, KIND_ORDER[j + 1], dif2_ready)
                        if j == 0 and is_back(i):
                            dve.wait_ge(mix1_done, PB * GROUPS * i)
                        if j % 2 == 0 and not (isinstance(i, int) and i <= 1):
                            dve.wait_ge(out_stored[j // 2], 16 * (i - 1))
                        outputs(0, stage0(i, j), j)
                    if isinstance(i, int) and i == 1:
                        for v in (2, 3):
                            dve.wait_ge(agg_stored[v], 16 * 2 * CHUNKS // STAGINGS)
                        sums(1, KIND_ORDER[PH - 1], dif2_ready)
                else:
                    for kind in KIND_ORDER[1:]:
                        sums(1, kind, dif2_ready)
                if is_back(i):
                    for j in range(PH):
                        if isinstance(i, int) and i == 1 and j < 2:
                            dve.wait_ge(agg_stored[j], 16 * 2 * CHUNKS // STAGINGS)
                        else:
                            dve.wait_ge(y2_low_ready, PH * (i - 1) + j - 1)
                        outputs(1, stage2(i - 1, j), j)
                if has(i, 1):
                    dve.wait_ge(phased, i + 3)
                    dve.wait_ge(kind_done, 4 * stage0(i, PH - 1) + 4)
                    for kind in KIND_ORDER:
                        sums(0, kind, dif0_ready)
                if is_front(i):
                    if not is_back(i):
                        dve.wait_ge(parts_stored[1], 16 * (PARTS + 1))
                        clear_edges(1)
                        dve.wait_ge(wino_ready[1], 1)
                    first_sums2(i)

            pipeline(dve, step)


def kernel(x, cond_128, fside_S_0, L0_cond_weight, L0_cond_c_weight, L1_cond_W0, L1_cond_b0, L1_cond_W1, L1_cond_b1,
           L1_cond_W2, L1_cond_b2, L1_cond_weight, L1_cond_bias_k, L2_cond_weight, L2_cond_c_weight, L3_cond_W0,
           L3_cond_b0, L3_cond_W1, L3_cond_b1, L3_cond_W2, L3_cond_b2, L3_cond_weight, L3_cond_bias_k):
    import numpy as np
    import concourse.bacc as bacc
    from concourse.bass_utils import run_bass_kernel_spmd

    nc = bacc.Bacc("TRN2", target_bir_lowering=False, num_devices=1)
    arrays = {}

    def give(name, a):
        a = np.ascontiguousarray(a)
        arrays[name] = a
        return nc.dram_tensor(name, a.shape, mybir.dt.from_np(a.dtype), kind="ExternalInput").ap()

    def taps(w):
        w = np.asarray(w)
        o, c, k = w.shape
        return w.reshape(o // c, c, c, k).transpose(3, 2, 0, 1)

    def expert_rows(w):
        w = np.asarray(w)
        return w[..., 0].transpose(0, 2, 1).reshape(w.shape[0], -1)

    def col(a):
        return np.asarray(a).reshape(-1, 1)

    x = np.asarray(x)
    p = x.shape[1]
    eye = np.eye(p, dtype=np.float32)
    wide = [np.asarray(cond_128).T, eye, eye.reshape(p, 4, -1)[:, ::-1].reshape(p, p), col(fside_S_0),
            np.asarray(L0_cond_c_weight).T, np.asarray(L2_cond_c_weight).T,
            L1_cond_W0, L1_cond_W1, L1_cond_W2, col(L1_cond_b0), col(L1_cond_b1),
            L3_cond_W0, L3_cond_W1, L3_cond_W2, col(L3_cond_b0), col(L3_cond_b1)]
    args = {
        "x": give("x", x),
        "wide": give("wide", np.concatenate([np.asarray(a) for a in wide], axis=1)),
        "bias_k": give("bias_k", np.stack([np.asarray(L1_cond_bias_k), np.asarray(L3_cond_bias_k)], axis=1)),
        "b2": give("b2", np.stack([np.asarray(L1_cond_b2), np.asarray(L3_cond_b2)])[None]),
        "experts": [give("experts_1", expert_rows(L1_cond_weight)), give("experts_3", expert_rows(L3_cond_weight))],
        "conv_w": [give("conv_w0", taps(L0_cond_weight)), give("conv_w2", taps(L2_cond_weight))],
        "out": nc.dram_tensor("out", x.shape, F32, kind="ExternalOutput").ap(),
    }
    conditioned_layers(nc, **args)
    r = run_bass_kernel_spmd(nc, [arrays], core_ids=[0])
    return r.results[0]["out"]
```
